# Optimizing a Trainium2 kernel written in Bass

```python
import numpy as np
import jax
import jax.numpy as jnp

def _softmax(x, axis=-1):
    return jax.nn.softmax(x, axis=axis)

def _gelu(x):
    return jax.nn.gelu(x, approximate=True)

def _silu(x):
    return jax.nn.silu(x)

def _sigmoid(x):
    return jax.nn.sigmoid(x)

def _layernorm(x, axis=-1, eps=1e-05):
    m = jnp.mean(x, axis=axis, keepdims=True)
    v = jnp.var(x, axis=axis, keepdims=True)
    return (x - m) / jnp.sqrt(v + eps)

def _scatter_add(tgt, idx, src, axis=0):
    return tgt.at[idx].add(src)

def _segment_sum(src, seg, n):
    return jax.ops.segment_sum(src, seg, n)
kernel_name = 'mk_seq_preln_d1_jaxref_r4_a3904e'

def setup_inputs(seed: int=0):
    np.random.seed(seed)
    _w = jnp.asarray

    def _L0_attn_setup():
        import jax, jax.numpy as jnp
        from jax import lax
        import numpy as np
        B, S, D = (4, 512, 256)
        D_INNER, D_STATE, D_CONV = (512, 16, 4)

        def silu(v):
            return v * jax.nn.sigmoid(v)
        key = jax.random.key(seed)
        ks = jax.random.split(key, 7)
        return {'x': jax.random.normal(ks[0], (B, S, D), jnp.float32), 'w_in': jax.random.normal(ks[1], (D, 2 * D_INNER), jnp.float32) * 0.02, 'conv_w': jax.random.normal(ks[2], (D_INNER, 1, D_CONV), jnp.float32) * 0.1, 'conv_b': jax.random.normal(ks[3], (D_INNER,), jnp.float32) * 0.01, 'w_B': jax.random.normal(ks[4], (D_INNER, D_STATE), jnp.float32) * 0.02, 'w_C': jax.random.normal(ks[5], (D_STATE, D_INNER), jnp.float32) * 0.02, 'w_out': jax.random.normal(ks[6], (D_INNER, D), jnp.float32) * 0.02}
    _L0_attn_in = _L0_attn_setup()

    def _L0_ffn_setup():
        import jax, jax.numpy as jnp
        import numpy as np
        TOP_K = 2
        key = jax.random.key(seed)
        ks = jax.random.split(key, 6)
        B, S, D, E = (8, 1024, 256, 8)
        s = 1.0 / np.sqrt(D)
        return {'x': jax.random.normal(ks[0], (B, S, D), dtype=jnp.float32), 'Wr': jax.random.normal(ks[1], (D, E), dtype=jnp.float32) * s, 'br': jnp.zeros((E,), dtype=jnp.float32), 'W1': jax.random.normal(ks[2], (E, D, D), dtype=jnp.float32) * s, 'b1': jnp.zeros((E, D), dtype=jnp.float32), 'W2': jax.random.normal(ks[3], (E, D, D), dtype=jnp.float32) * s, 'b2': jnp.zeros((E, D), dtype=jnp.float32)}
    _L0_ffn_in = _L0_ffn_setup()
    _d = {'L0_attn_x': _L0_attn_in['x'], 'L0_attn_w_in': _L0_attn_in['w_in'], 'L0_attn_conv_w': _L0_attn_in['conv_w'], 'L0_attn_conv_b': _L0_attn_in['conv_b'], 'L0_attn_w_B': _L0_attn_in['w_B'], 'L0_attn_w_C': _L0_attn_in['w_C'], 'L0_attn_w_out': _L0_attn_in['w_out'], 'L0_ffn_Wr': _L0_ffn_in['Wr'], 'L0_ffn_br': _L0_ffn_in['br'], 'L0_ffn_W1': _L0_ffn_in['W1'], 'L0_ffn_b1': _L0_ffn_in['b1'], 'L0_ffn_W2': _L0_ffn_in['W2'], 'L0_ffn_b2': _L0_ffn_in['b2']}
    _x0 = _d['L0_attn_x']
    _d['L0_attn_x'] = jax.random.normal(jax.random.fold_in(jax.random.key(seed), 1), (8, 1024, 256), dtype=_x0.dtype)
    del _x0
    return _d

def reference(L0_attn_x, L0_attn_w_in, L0_attn_conv_w, L0_attn_conv_b, L0_attn_w_B, L0_attn_w_C, L0_attn_w_out, L0_ffn_Wr, L0_ffn_br, L0_ffn_W1, L0_ffn_b1, L0_ffn_W2, L0_ffn_b2):

    def _L0_attn_ref(x, w_in, conv_w, conv_b, w_B, w_C, w_out):
        import jax, jax.numpy as jnp
        from jax import lax
        import numpy as np
        B, S, D = (4, 512, 256)
        D_INNER, D_STATE, D_CONV = (512, 16, 4)

        def silu(v):
            return v * jax.nn.sigmoid(v)
        d_inner = conv_w.shape[0]
        d_conv = conv_w.shape[2]
        xz = x @ w_in
        xp, z = jnp.split(xz, 2, axis=-1)
        xc = lax.conv_general_dilated(xp.transpose(0, 2, 1), conv_w, window_strides=(1,), padding=[(d_conv - 1, 0)], dimension_numbers=('NCH', 'OIH', 'NCH'), feature_group_count=d_inner)
        xc = (xc + conv_b[None, :, None]).transpose(0, 2, 1)
        xc = silu(xc)
        h0 = jnp.zeros((xc.shape[0], w_B.shape[1]), xc.dtype)

        def step(h, xt):
            h = h * 0.9 + 0.1 * (xt @ w_B)
            return (h, h @ w_C)
        _, ys = lax.scan(step, h0, xc.transpose(1, 0, 2))
        y = ys.transpose(1, 0, 2) * silu(z)
        return y @ w_out

    def _L0_ffn_ref(x, Wr, br, W1, b1, W2, b2):
        import jax, jax.numpy as jnp
        import numpy as np
        TOP_K = 2
        k = TOP_K
        scores0 = x[:, 0, :] @ Wr + br
        _, idx = jax.lax.top_k(scores0, k)
        W1g, b1g = (W1[idx], b1[idx])
        W2g, b2g = (W2[idx], b2[idx])
        h = jnp.einsum('bsd,bkde->bkse', x, W1g) + b1g[:, :, None, :]
        h = jax.nn.gelu(h, approximate=False)
        o = jnp.einsum('bkse,bkef->bksf', h, W2g) + b2g[:, :, None, :]
        return jnp.sum(o, axis=1) / k
    x = L0_attn_x
    x = x + _L0_attn_ref(_layernorm(x, axis=-1), L0_attn_w_in, L0_attn_conv_w, L0_attn_conv_b, L0_attn_w_B, L0_attn_w_C, L0_attn_w_out)
    x = x + _L0_ffn_ref(_layernorm(x, axis=-1), L0_ffn_Wr, L0_ffn_br, L0_ffn_W1, L0_ffn_b1, L0_ffn_W2, L0_ffn_b2)
    return x

_drawn_inputs = setup_inputs


def setup_inputs(seed=0):
    import zlib

    import numpy as np

    out = dict(_drawn_inputs(seed))
    spreads = {'L0_ffn_br': (0.0, 0.1), 'L0_ffn_b1': (0.0, 0.8), 'L0_ffn_b2': (0.0, 2.0)}
    factors = {'L0_attn_w_in': 8.0,
     'L0_attn_conv_w': 8.0,
     'L0_attn_conv_b': 8.0,
     'L0_attn_w_B': 8.0,
     'L0_attn_w_C': 8.0,
     'L0_attn_w_out': 8.0,
     'L0_ffn_Wr': 3.65,
     'L0_ffn_W1': 3.131,
     'L0_ffn_W2': 2.772}
    for name, (base, spread) in spreads.items():
        noise = np.random.default_rng([zlib.crc32(name.encode()), seed]).standard_normal(out[name].shape)
        drawn = base * np.exp(spread * noise) if base else spread * noise
        out[name] = jnp.asarray(drawn.astype(out[name].dtype))
    for name, factor in factors.items():
        out[name] = (out[name] * factor).astype(out[name].dtype)
    return out
```

```python
from contextlib import ExitStack

import concourse.bass as bass
from concourse import mybir

ALU = mybir.AluOpType
ACT = mybir.ActivationFunctionType
F32 = mybir.dt.float32
F32R = mybir.dt.float32r
U32 = mybir.dt.uint32

P = 128
DECAY, GAIN = 0.9, 0.1
EPS = 1e-5
TOP_K = 2


def build_block(nc, x, w_in, conv_w, conv_b, w_B, w_C, w_out, Wr, br, W1, b1, W2, b2, out):
    B, S, D = x.shape
    DI = w_out.shape[0]
    NST = w_B.shape[1]
    TAPS = conv_w.shape[2]
    E = Wr.shape[1]
    CH = 512
    PER = S // CH
    NC = B * PER
    TT = CH // P
    KD = D // P
    JD = DI // P
    JF = TOP_K * KD
    HALO = TAPS - 1
    REP = P // (2 * NST)
    assert PER == 2 and TT == 4 and KD == 2 and JD == 4 and JF == 4 and NST == 16 and E == 8

    x_t = x.rearrange("b s d -> (b s) d").rearrange("(c n p) d -> c p n d", p=P, n=TT)
    out_t = out.rearrange("b s d -> (b s) d").rearrange("(c n p) d -> c p n d", p=P, n=TT)

    with ExitStack() as ctx:
        def sb(name, shape, dt=F32):
            return ctx.enter_context(nc.sbuf_tensor(name, shape, dt))

        def sem(name):
            return ctx.enter_context(nc.semaphore(name))

        ident = sb("ident", [P, P])
        decay = sb("decay", [P, CH])
        w_in_hi, w_in_lo = sb("w_in_hi", [P, KD, 2 * DI], F32R), sb("w_in_lo", [P, KD, 2 * DI], F32R)
        w_out_hi, w_out_lo = sb("w_out_hi", [P, JD, D], F32R), sb("w_out_lo", [P, JD, D], F32R)
        b_mix = sb("b_mix", [P, JD, P], F32R)
        c_mix = sb("c_mix", [P, DI], F32R)
        c_raw = sb("c_raw", [P, DI])
        wb_raw = sb("wb_raw", [P, JD, NST])
        tap_w = sb("tap_w", [P, JD, TAPS])
        tap_b = sb("tap_b", [P, JD])
        w_router = sb("w_router", [P, KD, E])
        b_router = sb("b_router", [1, E])
        w1_all, w2_all = sb("w1_all", [P, E, KD * D]), sb("w2_all", [P, E, KD * D])
        b1_all = sb("b1_all", [P, E, KD])
        b2_all = sb("b2_all", [P, E, D])
        w1_hi, w1_lo = sb("w1_hi", [P, TOP_K, KD * D], F32R), sb("w1_lo", [P, TOP_K, KD * D], F32R)
        w2_hi, w2_lo = sb("w2_hi", [P, TOP_K, KD * D], F32R), sb("w2_lo", [P, TOP_K, KD * D], F32R)
        b1_sel = sb("b1_sel", [P, TOP_K, KD])
        b2_half = sb("b2_half", [P, D])
        b2_sel = sb("b2_sel", [P, D])
        scores = sb("scores", [1, E])
        best = sb("best", [1, 8])
        expert = sb("expert", [1, 8], U32)

        x_in = sb("x_in", [P, 2, TT, D])
        x_mid = sb("x_mid", [P, 2, TT, D])
        normed = sb("normed", [P, TT, D])
        stats = sb("stats", [P, TT, 6])
        mean_var = sb("mean_var", [P, TT, 2])
        neg_mean = sb("neg_mean", [P, TT])
        var_eps = sb("var_eps", [P, TT])
        minus_half = sb("minus_half", [P, TT])
        rstd = sb("rstd", [P, TT])
        xn1_hi, xn1_lo = sb("xn1_hi", [P, KD, CH], F32R), sb("xn1_lo", [P, KD, CH], F32R)
        xn2_hi, xn2_lo = sb("xn2_hi", [P, KD, CH], F32R), sb("xn2_lo", [P, KD, CH], F32R)
        first_tok = sb("first_tok", [P, KD])
        conv = sb("conv", [P, JD, S + HALO])
        part_hi, part_lo = sb("part_hi", [P, JD, CH], F32R), sb("part_lo", [P, JD, CH], F32R)
        gate = sb("gate", [P, JD, CH])
        state = sb("state", [P, 2, CH])
        state_mix = sb("state_mix", [P, CH], F32R)
        hid = sb("hid", [P, JF, CH])
        hid_hi, hid_lo = sb("hid_hi", [P, JF, CH], F32R), sb("hid_lo", [P, JF, CH], F32R)

        turn = [ctx.enter_context(nc.psum_tensor(f"turn{k}", [P, CH], F32)) for k in range(KD)]
        tok = [ctx.enter_context(nc.psum_tensor(f"tok{h}", [P, CH], F32)) for h in range(2)]
        blk = [ctx.enter_context(nc.psum_tensor(f"blk{j}", [P, CH], F32)) for j in range(JD)]

        w_loaded = sem("w_loaded")
        win_loaded = sem("win_loaded")
        e_loaded = sem("e_loaded")
        x_loaded = [sem("x_loaded0"), sem("x_loaded1")]
        consts_set = sem("consts_set")
        w_hi_set = sem("w_hi_set")
        w_lo_set = sem("w_lo_set")
        stats_ready = sem("stats_ready")
        stat_step = sem("stat_step")
        rstd_set = sem("rstd_set")
        norm_ready = sem("norm_ready")
        turned1, turned2 = sem("turned1"), sem("turned2")
        t1_hi, t1_lo = sem("t1_hi"), sem("t1_lo")
        t2_hi, t2_lo = sem("t2_hi"), sem("t2_lo")
        xp_ready = sem("xp_ready")
        tap_first = sem("tap_first")
        edge_set = sem("edge_set")
        tap_added = sem("tap_added")
        silu_set = sem("silu_set")
        xc_hi, xc_lo = sem("xc_hi"), sem("xc_lo")
        z_ready = sem("z_ready")
        gate_set = sem("gate_set")
        u_ready, scanned = sem("u_ready"), sem("scanned")
        h_hi, h_lo = sem("h_hi"), sem("h_lo")
        c_ready = sem("c_ready")
        y_set = sem("y_set")
        y_hi, y_lo = sem("y_hi"), sem("y_lo")
        mixed = sem("mixed")
        mid_set = sem("mid_set")
        b2_added = sem("b2_added")
        first_set = sem("first_set")
        scored = sem("scored")
        route_step = sem("route_step")
        e_hi, e_lo = sem("e_hi"), sem("e_lo")
        b_sel = sem("b_sel")
        up_ready = sem("up_ready")
        gelu_set = sem("gelu_set")
        g_hi, g_lo = sem("g_hi"), sem("g_lo")
        down_ready = sem("down_ready")
        done = sem("done")
        stored = [sem("stored0"), sem("stored1")]

        passed = sem("passed")

        NW = 7 + P // NST
        raw_in = hid
        raw_out = gate

        block = ctx.enter_context(nc.Block())

        def steps(eng, prologue, step, epilogue):
            prologue()
            with eng.Fori(0, NC // 2 - 1) as i:
                step(i * 2, 0, i, True)
                step(i * 2 + 1, 1, i, True)
            step(NC - 2, 0, NC // 2 - 1, False)
            epilogue()


        @block.sync
        def _(sp):
            sp.dma_start(x_in[:, 0], x_t[0]).then_inc(x_loaded[0], 16)
            for q in range(2):
                sp.sem_inc(stored[q], 16)
            sp.dma_start(raw_in[:].rearrange("p j c -> p (j c)").rearrange("p (k c) -> p k c", k=KD),
                         w_in.rearrange("(k p) c -> p k c", p=P)).then_inc(win_loaded, 16)
            sp.dma_start(raw_out[:].rearrange("p j c -> p (j c)")[:, 0:JD * D].rearrange("p (j c) -> p j c", j=JD),
                         w_out.rearrange("(j p) c -> p j c", p=P)).then_inc(win_loaded, 16)
            sp.dma_start(tap_w[:], conv_w.rearrange("(j p) o t -> p j (o t)", p=P)).then_inc(w_loaded, 16)
            with nc.allow_non_contiguous_dma(reason="small transposed loads, once"):
                sp.dma_start(tap_b[:], conv_b.rearrange("(j p) -> p j", p=P)).then_inc(w_loaded, 16)
                sp.dma_start(b1_all[:], b1.rearrange("e (k p) -> p e k", p=P)).then_inc(w_loaded, 16)
            sp.dma_start(wb_raw[:], w_B.rearrange("(j p) s -> p j s", p=P)).then_inc(w_loaded, 16)
            for r in range(P // NST):
                sp.dma_start(c_raw[r * NST:(r + 1) * NST, :], w_C).then_inc(w_loaded, 16)
            sp.dma_start(w_router[:], Wr.rearrange("(k p) e -> p k e", p=P)).then_inc(w_loaded, 16)
            sp.dma_start(b_router[:], br.rearrange("(o e) -> o e", o=1)).then_inc(w_loaded, 16)
            sp.dma_start(b2_all[:], b2.rearrange("(o e) d -> o e d", o=1).broadcast_to([P, E, D])).then_inc(w_loaded, 16)
            sp.dma_start(x_in[:, 1], x_t[1]).then_inc(x_loaded[1], 16)
            sp.dma_start(w1_all[:].rearrange("p e (k d) -> p e k d", k=KD),
                         W1.rearrange("e (k p) d -> p e k d", p=P)).then_inc(e_loaded, 16)
            sp.dma_start(w2_all[:].rearrange("p e (k d) -> p e k d", k=KD),
                         W2.rearrange("e (k p) d -> p e k d", p=P)).then_inc(e_loaded, 16)

            def store(f, q):
                sp.wait_ge(done, f * 2 + 2)
                sp.dma_start(out_t[f], x_mid[:, q]).then_inc(stored[q], 16)

            def fetch(c, q):
                sp.wait_ge(mid_set, c * 2 - 2)
                sp.dma_start(x_in[:, q], x_t[c]).then_inc(x_loaded[q], 16)

            fetch(2, 0)
            with sp.Fori(0, NC // 2 - 2) as i:
                store(i * 2, 0)
                fetch(i * 2 + 3, 1)
                store(i * 2 + 1, 1)
                fetch(i * 2 + 4, 0)
            store(NC - 4, 0)
            fetch(NC - 1, 1)
            store(NC - 3, 1)
            store(NC - 2, 0)
            store(NC - 1, 1)
            for q in range(2):
                sp.wait_ge(stored[q], 16 * (NC // 2 + 1))

        @block.gpsimd
        def _(pool):
            nc.gpsimd.memset(ident[:], 0.0).then_inc(consts_set, 1)
            nc.gpsimd.memset(decay[:], DECAY).then_inc(consts_set, 1)
            nc.gpsimd.memset(minus_half[:], -0.5).then_inc(consts_set, 1)
            pool.wait_ge(consts_set, 3)
            nc.gpsimd.affine_select(out=ident[:], in_=ident[:], compare_op=ALU.not_equal, fill=1.0, base=0,
                                    pattern=[[-1, P]], channel_multiplier=1).then_inc(consts_set, 1)
            pool.wait_ge(consts_set, 4)

            def normalise(src, ln):
                pool.wait_ge(stats_ready, ln + 1)
                nc.gpsimd.tensor_tensor(rstd[:], var_eps[:], minus_half[:], ALU.pow).then_inc(rstd_set, 1)
                pool.wait_ge(rstd_set, ln + 1)
                pool.sem_inc(passed, 1)
                for n in range(TT):
                    ins = nc.gpsimd.tensor_scalar(normed[:, n, :], src[:, n, :], neg_mean[:, n:n + 1],
                                                  rstd[:, n:n + 1], ALU.add, ALU.mult)
                ins.then_inc(norm_ready, 1)

            def split_conv(a, qa):
                for j in range(JD):
                    pool.wait_ge(xc_hi, a * JD + j + 1)
                    cols = conv[:, j, qa * CH:(qa + 1) * CH]
                    nc.gpsimd.tensor_tensor(part_lo[:, j, :], cols, part_hi[:, j, :].bitcast(F32),
                                            ALU.subtract).then_inc(xc_lo, 1)

            def split_hidden(f):
                for j in range(JF):
                    pool.wait_ge(g_hi, f * JF + j + 1)
                    nc.gpsimd.tensor_tensor(hid_lo[:, j, :], hid[:, j, :], hid_hi[:, j, :].bitcast(F32),
                                            ALU.subtract).then_inc(g_lo, 1)

            def add_b2(f, q):
                pool.wait_ge(b_sel, (f - q) * 2 + 4)
                for n in range(TT):
                    ins = nc.gpsimd.tensor_tensor(x_mid[:, q, n, :], x_mid[:, q, n, :], b2_sel[:], ALU.add)
                ins.then_inc(b2_added, 1)

            def prologue():
                normalise(x_in[:, 0], 0)
                split_conv(0, 0)
                pool.wait_ge(turned1, KD)
                normalise(x_in[:, 1], 1)

            def step(f, q, seq, more):
                pool.wait_ge(turned1, f * KD + 2 * KD)
                normalise(x_mid[:, q], f * 2 + 2)
                split_conv(f + 1, 1 - q)
                add_b2(f, q)
                split_hidden(f)
                if more:
                    pool.wait_ge(turned2, f * KD + KD)
                    normalise(x_in[:, q], f * 2 + 3)

            def epilogue():
                f = NC - 1
                normalise(x_mid[:, 1], 2 * NC - 1)
                add_b2(f, 1)
                split_hidden(f)

            steps(pool, prologue, step, epilogue)

        @block.scalar
        def _(act):
            def hi(dst, src, scale=1.0):
                return nc.scalar.activation(dst, src, ACT.Copy, scale=scale)

            act.wait_ge(win_loaded, 32)
            hi(w_in_hi[:].rearrange("p k c -> p (k c)"), raw_in[:].rearrange("p j c -> p (j c)")).then_inc(w_hi_set, 1)
            hi(w_out_hi[:].rearrange("p k c -> p (k c)"),
               raw_out[:].rearrange("p j c -> p (j c)")[:, 0:JD * D]).then_inc(w_hi_set, 1)
            act.wait_ge(w_loaded, 16 * NW)
            nc.scalar.activation(state[:, 0, :], c_raw[:], ACT.Copy, scale=GAIN).then_inc(w_hi_set, 1)
            act.wait_ge(w_hi_set, 3)
            hi(c_mix[:], state[:, 0, :]).then_inc(w_hi_set, 1)
            for r in range(REP):
                hi(b_mix[:, :, 2 * r * NST:(2 * r + 1) * NST], wb_raw[:]).then_inc(w_hi_set, 1)

            def turn_hi1(c):
                for k in range(KD):
                    act.wait_ge(turned1, c * KD + k + 1)
                    hi(xn1_hi[:, k, :], turn[k][:]).then_inc(t1_hi, 1)

            def turn_hi2(f, q):
                for k in range(KD):
                    act.wait_ge(turned2, f * KD + k + 1)
                    if q == 0:
                        hi(first_tok[:, k:k + 1], turn[k][:, 0:1]).then_inc(first_set, 1)
                    hi(xn2_hi[:, k, :], turn[k][:]).then_inc(t2_hi, 1)

            def first_taps(a, qa):
                for j in range(JD):
                    act.wait_ge(xp_ready, a * JD + j + 1)
                    lo = qa * CH + HALO
                    nc.scalar.activation(conv[:, j, lo:lo + CH], blk[j][:], ACT.Identity, bias=tap_b[:, j:j + 1],
                                         scale=tap_w[:, j, 0:1]).then_inc(tap_first, 1)

            def gates(a, qa):
                for j in range(JD):
                    act.wait_ge(tap_added, a * JD * HALO + (j // 2 + 1) * 2 * HALO)
                    cols = conv[:, j, qa * CH:(qa + 1) * CH]
                    nc.scalar.activation(cols, cols, ACT.Silu).then_inc(silu_set, 1)
                    act.wait_ge(z_ready, a * JD + j + 1)
                    nc.scalar.activation(gate[:, j, :], blk[j][:], ACT.Silu).then_inc(gate_set, 1)
                    act.wait_ge(silu_set, a * JD + j + 1)
                    hi(part_hi[:, j, :], cols).then_inc(xc_hi, 1)

            def choose(f, e0, e1):
                for t, e in enumerate((e0, e1)):
                    hi(w1_hi[:, t, :], w1_all[:, bass.ds(e, 1), :].rearrange("p o c -> p (o c)")).then_inc(e_hi, 1)
                for t, e in enumerate((e0, e1)):
                    hi(w2_hi[:, t, :], w2_all[:, bass.ds(e, 1), :].rearrange("p o c -> p (o c)"), 1.0 / TOP_K).then_inc(e_hi, 1)

            def route(f, seq):
                act.wait_ge(route_step, seq * 3 + 3)
                act.sem_inc(passed, 1)
                e0 = nc.scalar.value_load(expert[0:1, 0:1], min_val=0, max_val=E - 1)
                e1 = nc.scalar.value_load(expert[0:1, 1:2], min_val=0, max_val=E - 1)
                choose(f, e0, e1)

            def gelus(f):
                for j in range(JF):
                    act.wait_ge(up_ready, f * JF + j + 1)
                    nc.scalar.activation(hid[:, j, :], blk[j][:], ACT.Gelu,
                                         bias=b1_sel[:, j // KD, j % KD:j % KD + 1]).then_inc(gelu_set, 1)
                    act.wait_ge(gelu_set, f * JF + j + 1)
                    hi(hid_hi[:, j, :], hid[:, j, :]).then_inc(g_hi, 1)

            def state_hi(a, qa):
                act.wait_ge(scanned, a + 1)
                hi(state_mix[:], state[:, qa, :]).then_inc(h_hi, 1)

            def ys(a):
                for j in range(JD):
                    act.wait_ge(y_set, a * JD + j + 1)
                    hi(part_hi[:, j, :], gate[:, j, :]).then_inc(y_hi, 1)

            def prologue():
                turn_hi1(0)
                act.wait_ge(w_lo_set, 3 + REP)
                first_taps(0, 0)
                gates(0, 0)
                state_hi(0, 0)
                turn_hi1(1)
                ys(0)

            def step(f, q, seq, more):
                first_taps(f + 1, 1 - q)
                turn_hi2(f, q)
                gates(f + 1, 1 - q)
                if q == 0:
                    act.wait_ge(e_loaded, 32)
                    route(f, seq)
                gelus(f)
                state_hi(f + 1, 1 - q)
                ys(f + 1)
                if more:
                    turn_hi1(f + 2)

            def epilogue():
                turn_hi2(NC - 1, 1)
                gelus(NC - 1)

            steps(act, prologue, step, epilogue)

        @block.vector
        def _(dve):
            def lo(dst, src, hi):
                return nc.vector.tensor_tensor(dst, src, hi.bitcast(F32), ALU.subtract)

            dve.wait_ge(w_hi_set, 1)
            lo(w_in_lo[:].rearrange("p k c -> p (k c)"), raw_in[:].rearrange("p j c -> p (j c)"),
               w_in_hi[:].rearrange("p k c -> p (k c)")).then_inc(w_lo_set, 1)
            dve.wait_ge(w_hi_set, 2)
            lo(w_out_lo[:].rearrange("p k c -> p (k c)"), raw_out[:].rearrange("p j c -> p (j c)")[:, 0:JD * D],
               w_out_hi[:].rearrange("p k c -> p (k c)")).then_inc(w_lo_set, 1)
            dve.wait_ge(w_hi_set, 4 + REP)
            for r in range(REP):
                lo(b_mix[:, :, (2 * r + 1) * NST:(2 * r + 2) * NST], wb_raw[:],
                   b_mix[:, :, 2 * r * NST:(2 * r + 1) * NST]).then_inc(w_lo_set, 1)
            for r in (32, 96):
                lo(c_mix[r:r + 32, :], state[r:r + 32, 0, :], c_mix[r:r + 32, :]).then_inc(w_lo_set, 1)

            def statistics(src, ln, mid=None):
                if not (isinstance(ln, int) and ln == 0):
                    dve.wait_ge(norm_ready, ln)
                for n in range(TT):
                    if mid is not None and n % 2 == 0:
                        dve.wait_ge(mid_set, mid * 2 + n // 2 + 1)
                    ins = nc.vector.bn_stats(stats[:, n, :], src[:, n, :])
                ins.then_inc(stat_step, 1)
                dve.wait_ge(stat_step, ln * 2 + 1)
                dve.sem_inc(passed, 1)
                for n in range(TT):
                    ins = nc.vector.bn_aggr(mean_var[:, n, :], stats[:, n, :])
                ins.then_inc(stat_step, 1)
                dve.wait_ge(stat_step, ln * 2 + 2)
                nc.vector.tensor_scalar(neg_mean[:], mean_var[:, :, 0], -1.0, None, ALU.mult)
                nc.vector.tensor_scalar(var_eps[:], mean_var[:, :, 1], EPS, None, ALU.add).then_inc(stats_ready, 1)

            def turn_lo(c, hi_sem, lo_sem, hi_t, lo_t):
                for k in range(KD):
                    dve.wait_ge(hi_sem, c * KD + k + 1)
                    lo(lo_t[:, k, :], turn[k][:], hi_t[:, k, :]).then_inc(lo_sem, 1)

            def taps(a, qa, pair):
                for t in range(1, TAPS):
                    for jj in range(2):
                        j = 2 * pair + jj
                        if t == 1:
                            dve.wait_ge(tap_first, a * JD + j + 1)
                        else:
                            dve.wait_ge(tap_added, a * JD * HALO + pair * 2 * HALO + (t - 2) * 2 + jj + 1)
                        at = qa * CH + HALO - t
                        cols = conv[:, j, at:at + CH]
                        nc.vector.scalar_tensor_tensor(cols, blk[j][:], tap_w[:, j, t:t + 1], cols, ALU.mult,
                                                       ALU.add).then_inc(tap_added, 1)

            def scan(a, qa):
                dve.wait_ge(u_ready, a + 1)
                start = 0.0 if qa == 0 else state[:, 0, CH - 1:CH]
                nc.vector.tensor_tensor_scan(state[:, qa, :], decay[:], turn[0][:], start, ALU.mult,
                                             ALU.add).then_inc(scanned, 1)

            def state_lo(a, qa):
                dve.wait_ge(h_hi, a + 1)
                lo(state_mix[P // 2:P, :], state[P // 2:P, qa, :], state_mix[P // 2:P, :]).then_inc(h_lo, 1)

            def ys(a, j):
                dve.wait_ge(c_ready, a * JD + j + 1)
                nc.vector.tensor_tensor(gate[:, j, :], blk[j][:], gate[:, j, :], ALU.mult).then_inc(y_set, 1)

            def ys_lo(a, j):
                dve.wait_ge(y_hi, a * JD + j + 1)
                lo(part_lo[:, j, :], gate[:, j, :], part_hi[:, j, :]).then_inc(y_lo, 1)

            def y_all(a):
                ys(a, 0)
                for j in range(JD):
                    if j + 1 < JD:
                        ys(a, j + 1)
                    ys_lo(a, j)

            def residual(a, qa, seq):
                dve.wait_ge(stored[qa], seq * 16 + 16)
                dve.wait_ge(mixed, a + 1)
                for h in range(2):
                    rows = x_mid[:, qa, 2 * h:2 * h + 2, :].rearrange("p n d -> p (n d)")
                    nc.vector.tensor_tensor(rows, tok[h][:], x_in[:, qa, 2 * h:2 * h + 2, :]
                                            .rearrange("p n d -> p (n d)"), ALU.add).then_inc(mid_set, 1)

            def finish(f, q, h):
                dve.wait_ge(down_ready, f * 2 + h + 1)
                dve.wait_ge(b2_added, f + 1)
                rows = x_mid[:, q, 2 * h:2 * h + 2, :].rearrange("p n d -> p (n d)")
                nc.vector.tensor_tensor(rows, tok[h][:], rows, ALU.add).then_inc(done, 1)

            def choose(f, seq):
                dve.wait_ge(scored, seq + 1)
                nc.vector.tensor_tensor(scores[:], tok[0][0:1, 0:E], b_router[:], ALU.add).then_inc(route_step, 1)
                dve.wait_ge(route_step, seq * 3 + 1)
                dve.sem_inc(passed, 1)
                nc.vector.max(best[:], scores[:]).then_inc(route_step, 1)
                dve.wait_ge(route_step, seq * 3 + 2)
                dve.sem_inc(passed, 1)
                nc.vector.max_index(expert[:], best[:], scores[:]).then_inc(route_step, 1)
                dve.wait_ge(route_step, seq * 3 + 3)
                dve.sem_inc(passed, 1)
                e0 = nc.vector.value_load(expert[0:1, 0:1], min_val=0, max_val=E - 1)
                e1 = nc.vector.value_load(expert[0:1, 1:2], min_val=0, max_val=E - 1)
                nc.vector.tensor_copy(b1_sel[:, 0, :], b1_all[:, bass.ds(e0, 1), :].rearrange("p o k -> p (o k)"))
                nc.vector.tensor_copy(b1_sel[:, 1, :], b1_all[:, bass.ds(e1, 1), :].rearrange("p o k -> p (o k)")
                                      ).then_inc(b_sel, 1)
                nc.vector.tensor_scalar(b2_half[:], b2_all[:, bass.ds(e0, 1), :].rearrange("p o d -> p (o d)"),
                                        1.0 / TOP_K, None, ALU.mult).then_inc(b_sel, 1)
                dve.wait_ge(b_sel, f * 2 + 2)
                nc.vector.scalar_tensor_tensor(b2_sel[:], b2_all[:, bass.ds(e1, 1), :].rearrange("p o d -> p (o d)"),
                                               1.0 / TOP_K, b2_half[:], ALU.mult, ALU.add).then_inc(b_sel, 2)
                n = 0
                for raw, his, los, scale in ((w1_all, w1_hi, w1_lo, 1.0), (w2_all, w2_hi, w2_lo, 1.0 / TOP_K)):
                    for t, e in enumerate((e0, e1)):
                        n += 1
                        dve.wait_ge(e_hi, f * 2 + n)
                        nc.vector.scalar_tensor_tensor(
                            los[:, t, :], raw[:, bass.ds(e, 1), :].rearrange("p o c -> p (o c)"), scale,
                            his[:, t, :].bitcast(F32), ALU.mult, ALU.subtract).then_inc(e_lo, 1)

            def begin(a, seq):
                nc.vector.tensor_copy(conv[:, :, 0:HALO], tap_b[:].rearrange("p (j o) -> p j o", o=1)
                                      .broadcast_to([P, JD, HALO])).then_inc(edge_set, 1)
                dve.wait_ge(edge_set, seq + 1)

            def prologue():
                dve.wait_ge(x_loaded[0], 16)
                statistics(x_in[:, 0], 0)
                dve.wait_ge(w_loaded, 16 * NW)
                begin(0, 0)
                turn_lo(0, t1_hi, t1_lo, xn1_hi, xn1_lo)
                taps(0, 0, 0)
                taps(0, 0, 1)
                dve.wait_ge(x_loaded[1], 16)
                statistics(x_in[:, 1], 1)
                dve.wait_ge(consts_set, 4)
                scan(0, 0)
                state_lo(0, 0)
                turn_lo(1, t1_hi, t1_lo, xn1_hi, xn1_lo)
                y_all(0)
                residual(0, 0, 0)
                statistics(x_mid[:, 0], 2, 0)

            def step(f, q, seq, more):
                a, qa = f + 1, 1 - q
                if q == 1:
                    begin(a, seq + 1)
                taps(a, qa, 0)
                turn_lo(f, t2_hi, t2_lo, xn2_hi, xn2_lo)
                taps(a, qa, 1)
                if q == 0:
                    dve.wait_ge(e_loaded, 32)
                    choose(f, seq)
                if more:
                    dve.wait_ge(x_loaded[q], (seq + 2) * 16)
                    statistics(x_in[:, q], f * 2 + 3)
                scan(a, qa)
                state_lo(a, qa)
                finish(f, q, 0)
                y_all(a)
                finish(f, q, 1)
                residual(a, qa, seq + q)
                if more:
                    turn_lo(f + 2, t1_hi, t1_lo, xn1_hi, xn1_lo)
                statistics(x_mid[:, qa], f * 2 + 4 if more else f * 2 + 3, a)

            def epilogue():
                f = NC - 1
                turn_lo(f, t2_hi, t2_lo, xn2_hi, xn2_lo)
                finish(f, 1, 0)
                finish(f, 1, 1)

            steps(dve, prologue, step, epilogue)

        @block.tensor
        def _(pe):
            mm = nc.tensor.matmul

            def turns(c, ready, n, sem_out):
                pe.wait_ge(norm_ready, n)
                for k in range(KD):
                    for t in range(TT):
                        ins = nc.tensor.transpose(turn[k][:, t * P:(t + 1) * P], normed[:, t, k * P:(k + 1) * P],
                                                  ident[:])
                    ins.then_inc(sem_out, 1)

            def project(dst, whi, wlo, his, los, los_ready, c, sem_out):
                for k in range(KD):
                    mm(dst, whi(k), his[:, k, :], start=(k == 0), stop=False)
                    mm(dst, wlo(k), his[:, k, :], start=False, stop=False)
                for k in range(KD):
                    if los_ready is not None:
                        pe.wait_ge(los_ready, c * KD + k + 1)
                    ins = mm(dst, whi(k), los[:, k, :], start=False, stop=(k == KD - 1))
                ins.then_inc(sem_out, 1)

            def in_proj(a, j, part, sem_out):
                c0 = part * DI + j * P
                project(blk[j][:], lambda k: w_in_hi[:, k, c0:c0 + P], lambda k: w_in_lo[:, k, c0:c0 + P],
                        xn1_hi, xn1_lo, t1_lo if part == 0 and j == 0 else None, a, sem_out)

            def xp(a):
                pe.wait_ge(t1_hi, a * KD + KD)
                for j in range(JD):
                    if not (isinstance(a, int) and a == 0):
                        pe.wait_ge(y_set, a * JD - JD + j + 1)
                    in_proj(a, j, 0, xp_ready)

            def z(a, between=None):
                for j in range(JD):
                    pe.wait_ge(tap_added, a * JD * HALO + (j // 2) * 2 * HALO + 2 * (HALO - 1) + j % 2 + 1)
                    in_proj(a, j, 1, z_ready)
                    if j == 0 and between is not None:
                        between()

            def up(f, q, seq):
                pe.wait_ge(t2_hi, f * KD + KD)
                if q == 0:
                    pe.wait_ge(e_lo, seq * 4 + 2)
                for j in range(JF):
                    if not (isinstance(f, int) and f == NC - 1):
                        pe.wait_ge(gate_set, f * JD + JD + j + 1)
                    t, m = j // KD, j % KD

                    def w(part, k, t=t, m=m):
                        return part[:, t, k * D + m * P:k * D + (m + 1) * P]
                    project(blk[j][:], lambda k: w(w1_hi, k), lambda k: w(w1_lo, k), xn2_hi, xn2_lo,
                            t2_lo if j == 0 else None, f, up_ready)

            def down(f, h):
                for j in range(JF):
                    if h == 0:
                        pe.wait_ge(g_lo, f * JF + j + 1)
                    t, k = j // KD, j % KD
                    for nn in range(2):
                        rows = slice((2 * h + nn) * P, (2 * h + nn + 1) * P)
                        dst = tok[h][:, nn * D:(nn + 1) * D]
                        cols = slice(k * D, (k + 1) * D)
                        mm(dst, hid_hi[:, j, rows], w2_hi[:, t, cols], start=(j == 0 and nn == 0), stop=False,
                           skip_group_check=True)
                        mm(dst, hid_hi[:, j, rows], w2_lo[:, t, cols], start=False, stop=False, skip_group_check=True)
                        ins = mm(dst, hid_lo[:, j, rows], w2_hi[:, t, cols], start=False, stop=(j == JF - 1 and nn == 1),
                                 skip_group_check=True)
                ins.then_inc(down_ready, 1)

            def state_in(a):
                for part, ready in ((part_hi, xc_hi), (part_lo, xc_lo)):
                    for j in range(JD):
                        pe.wait_ge(ready, a * JD + j + 1)
                        ins = mm(turn[0][:], b_mix[:, j, :], part[:, j, :], start=(part is part_hi and j == 0),
                                 stop=(part is part_lo and j == JD - 1))
                ins.then_inc(u_ready, 1)

            def state_out(a, after):
                pe.wait_ge(h_lo, a + 1)
                for j in range(JD):
                    after(j)
                    mm(blk[j][:], c_mix[:, j * P:(j + 1) * P], state_mix[:], start=True,
                       stop=True).then_inc(c_ready, 1)

            def out_proj(a):
                for j in range(JD):
                    pe.wait_ge(y_lo, a * JD + j + 1)
                    for n in range(TT):
                        rows = slice(n * P, (n + 1) * P)
                        dst = tok[n // 2][:, (n % 2) * D:(n % 2 + 1) * D]
                        mm(dst, part_hi[:, j, rows], w_out_hi[:, j, :], start=(j == 0 and n % 2 == 0), stop=False,
                           skip_group_check=True)
                        mm(dst, part_hi[:, j, rows], w_out_lo[:, j, :], start=False, stop=False, skip_group_check=True)
                        ins = mm(dst, part_lo[:, j, rows], w_out_hi[:, j, :], start=False,
                                 stop=(j == JD - 1 and n % 2 == 1), skip_group_check=True)
                ins.then_inc(mixed, 1)

            def prologue():
                pe.wait_ge(consts_set, 4)
                turns(0, None, 1, turned1)
                pe.wait_ge(w_lo_set, 4 + REP)
                xp(0)
                z(0)
                state_in(0)
                pe.wait_ge(scanned, 1)
                turns(1, None, 2, turned1)
                state_out(0, lambda j: pe.wait_ge(gate_set, j + 1))
                out_proj(0)

            def step(f, q, seq, more):
                a = f + 1
                xp(a)
                turns(f, None, f * 2 + 3, turned2)

                def score():
                    pe.wait_ge(first_set, seq * KD + KD)
                    pe.wait_ge(mid_set, f * 2 + 2)
                    for k in range(KD):
                        ins = mm(tok[0][0:1, 0:E], first_tok[:, k:k + 1], w_router[:, k, :], start=(k == 0),
                                 stop=(k == KD - 1))
                    ins.then_inc(scored, 1)
                z(a, score if q == 0 else None)
                up(f, q, seq)
                state_in(a)
                if q == 0:
                    pe.wait_ge(e_lo, seq * 4 + 4)
                pe.wait_ge(mid_set, f * 2 + 2)
                down(f, 0)
                if more:
                    pe.wait_ge(scanned, a + 1)
                    turns(f + 2, None, f * 2 + 4, turned1)
                state_out(a, lambda j: None)
                down(f, 1)
                pe.wait_ge(done, f * 2 + 2)
                out_proj(a)

            def epilogue():
                f = NC - 1
                turns(f, None, 2 * NC, turned2)
                pe.wait_ge(y_set, NC * JD)
                up(f, 1, None)
                pe.wait_ge(mid_set, 2 * NC)
                down(f, 0)
                down(f, 1)

            steps(pe, prologue, step, epilogue)


_INS = ["L0_attn_x", "L0_attn_w_in", "L0_attn_conv_w", "L0_attn_conv_b", "L0_attn_w_B", "L0_attn_w_C",
        "L0_attn_w_out", "L0_ffn_Wr", "L0_ffn_br", "L0_ffn_W1", "L0_ffn_b1", "L0_ffn_W2", "L0_ffn_b2"]


def kernel(**inputs):
    import numpy as _np
    import concourse.bacc as _bacc
    from concourse import mybir as _mybir
    from concourse.bass_utils import run_bass_kernel_spmd as _run

    nc = _bacc.Bacc("TRN2", target_bir_lowering=False, num_devices=1)
    arrays, args = {}, []
    for name in _INS:
        a = _np.ascontiguousarray(inputs[name])
        arrays[f"in_{name}"] = a
        args.append(nc.dram_tensor(f"in_{name}", a.shape, _mybir.dt.from_np(a.dtype), kind="ExternalInput").ap())
    shape = inputs["L0_attn_x"].shape
    args.append(nc.dram_tensor("out_0", shape, F32, kind="ExternalOutput").ap())
    build_block(nc, *args)
    r = _run(nc, [arrays], core_ids=[0])
    return r.results[0]["out_0"]
```

```python
from contextlib import ExitStack

import concourse.bass as bass
from concourse import mybir

ALU = mybir.AluOpType
ACT = mybir.ActivationFunctionType
F32 = mybir.dt.float32
F32R = mybir.dt.float32r
U32 = mybir.dt.uint32

P = 128
DECAY, GAIN = 0.9, 0.1
EPS = 1e-5
TOP_K = 2


def build_block(nc, x, w_in, conv_w, conv_b, w_B, w_C, w_out, Wr, br, W1, b1, W2, b2, out):
    B, S, D = x.shape
    DI = w_out.shape[0]
    NST = w_B.shape[1]
    TAPS = conv_w.shape[2]
    E = Wr.shape[1]
    CH = 512
    PER = S // CH
    NC = B * PER
    TT = CH // P
    KD = D // P
    JD = DI // P
    JF = TOP_K * KD
    HALO = TAPS - 1
    REP = P // (2 * NST)
    assert PER == 2 and TT == 4 and KD == 2 and JD == 4 and JF == 4 and NST == 16 and E == 8

    x_t = x.rearrange("b s d -> (b s) d").rearrange("(c n p) d -> c p n d", p=P, n=TT)
    out_t = out.rearrange("b s d -> (b s) d").rearrange("(c n p) d -> c p n d", p=P, n=TT)

    with ExitStack() as ctx:
        def sb(name, shape, dt=F32):
            return ctx.enter_context(nc.sbuf_tensor(name, shape, dt))

        def sem(name):
            return ctx.enter_context(nc.semaphore(name))

        ident = sb("ident", [P, P])
        decay = sb("decay", [P, CH])
        w_in_hi, w_in_lo = sb("w_in_hi", [P, KD, 2 * DI], F32R), sb("w_in_lo", [P, KD, 2 * DI], F32R)
        w_out_hi, w_out_lo = sb("w_out_hi", [P, JD, D], F32R), sb("w_out_lo", [P, JD, D], F32R)
        b_mix = sb("b_mix", [P, JD, P], F32R)
        c_mix = sb("c_mix", [P, DI], F32R)
        wb_raw = sb("wb_raw", [P, JD, NST])
        tap_w = sb("tap_w", [P, JD, TAPS])
        tap_b = sb("tap_b", [P, JD])
        w_router = sb("w_router", [P, KD, E])
        b_router = sb("b_router", [1, E])
        w1_all, w2_all = sb("w1_all", [P, E, KD * D]), sb("w2_all", [P, E, KD * D])
        b1_all = sb("b1_all", [P, E, KD])
        b2_all = sb("b2_all", [P, E, D])
        w1_hi, w1_lo = sb("w1_hi", [P, TOP_K, KD * D], F32R), sb("w1_lo", [P, TOP_K, KD * D], F32R)
        w2_hi, w2_lo = sb("w2_hi", [P, TOP_K, KD * D], F32R), sb("w2_lo", [P, TOP_K, KD * D], F32R)
        b1_sel = sb("b1_sel", [P, TOP_K, KD])
        b2_half = sb("b2_half", [P, D])
        b2_sel = sb("b2_sel", [P, D])
        scores = sb("scores", [1, E])
        best = sb("best", [1, 8])
        expert = sb("expert", [1, 8], U32)

        x_in = sb("x_in", [P, TT, D])
        x_mid = sb("x_mid", [P, 2, TT, D])
        normed = sb("normed", [P, TT, D])
        stats1_t, stats2_t = sb("stats1_t", [P, TT, 6]), sb("stats2_t", [P, TT, 6])
        mean_var1, mean_var2 = sb("mean_var1", [P, TT, 2]), sb("mean_var2", [P, TT, 2])
        var_eps1, var_eps2 = sb("var_eps1", [P, TT]), sb("var_eps2", [P, TT])
        rstd1, rstd2 = sb("rstd1", [P, TT]), sb("rstd2", [P, TT])
        neg_mean = sb("neg_mean", [P, TT])
        minus_half = sb("minus_half", [P, TT])
        xn1_hi, xn1_lo = sb("xn1_hi", [P, 2, KD, CH], F32R), sb("xn1_lo", [P, 2, KD, CH], F32R)
        xn2_hi, xn2_lo = sb("xn2_hi", [P, KD, CH], F32R), sb("xn2_lo", [P, KD, CH], F32R)
        first_tok = sb("first_tok", [P, KD])
        conv = sb("conv", [P, JD, CH + HALO])
        xc_hi, xc_lo = sb("xc_hi", [P, JD, CH], F32R), sb("xc_lo", [P, JD, CH], F32R)
        gate = sb("gate", [P, JD, CH])
        y_hi, y_lo = sb("y_hi", [P, JD, CH], F32R), sb("y_lo", [P, JD, CH], F32R)
        state = sb("state", [P, 2, CH])
        state_mix = sb("state_mix", [P, CH], F32R)
        hid = sb("hid", [P, 2, CH])
        hid_hi, hid_lo = sb("hid_hi", [P, JF, CH], F32R), sb("hid_lo", [P, JF, CH], F32R)

        turn = [ctx.enter_context(nc.psum_tensor(f"turn{k}", [P, CH], F32)) for k in range(KD)]
        tok = [ctx.enter_context(nc.psum_tensor(f"tok{h}", [P, CH], F32)) for h in range(2)]
        blk = [ctx.enter_context(nc.psum_tensor(f"blk{j}", [P, CH], F32)) for j in range(JD)]

        w_loaded = sem("w_loaded")
        win_loaded = sem("win_loaded")
        e_loaded = sem("e_loaded")
        x_loaded = sem("x_loaded")
        res_loaded = [sem("res_loaded0"), sem("res_loaded1")]
        consts_set = sem("consts_set")
        w_hi_set = sem("w_hi_set")
        w_lo_set = sem("w_lo_set")
        stat1_step, stat2_step = sem("stat1_step"), sem("stat2_step")
        stats1_ready = sem("stats1_ready")
        stats2_ready = sem("stats2_ready")
        rstd1_set, rstd2_set = sem("rstd1_set"), sem("rstd2_set")
        norm1_ready = sem("norm1_ready")
        norm2_ready = sem("norm2_ready")
        turned1, turned2 = sem("turned1"), sem("turned2")
        turned_first = sem("turned_first")
        t1_hi, t1_lo = sem("t1_hi"), sem("t1_lo")
        t2_hi, t2_lo = sem("t2_hi"), sem("t2_lo")
        xp_ready = sem("xp_ready")
        tap_first = sem("tap_first")
        edge_set = sem("edge_set")
        tap_added = sem("tap_added")
        silu_set = sem("silu_set")
        xc_hi_set, xc_lo_set = sem("xc_hi_set"), sem("xc_lo_set")
        z_ready = sem("z_ready")
        gate_set = sem("gate_set")
        u_ready, scanned = sem("u_ready"), sem("scanned")
        h_hi, h_lo = sem("h_hi"), sem("h_lo")
        c_ready = sem("c_ready")
        y_set = sem("y_set")
        y_hi_set, y_lo_set = sem("y_hi_set"), sem("y_lo_set")
        mixed = sem("mixed")
        mid_set = sem("mid_set")
        b2_added = sem("b2_added")
        first_set = sem("first_set")
        scored = sem("scored")
        route_step = sem("route_step")
        e_hi, e_lo = sem("e_hi"), sem("e_lo")
        b_sel = sem("b_sel")
        up_ready = sem("up_ready")
        gelu_set = sem("gelu_set")
        g_hi, g_lo = sem("g_hi"), sem("g_lo")
        down_ready = sem("down_ready")
        done = sem("done")
        stored = [sem("stored0"), sem("stored1")]
        passed = sem("passed")

        NW = 7 + P // NST
        raw_in, raw_out, raw_c = gate[:], hid[:], conv[:, 0, 0:DI]

        block = ctx.enter_context(nc.Block())

        def steps(eng, prologue, step, epilogue):
            prologue()
            with eng.Fori(0, NC // 2 - 2) as i:
                step(i * 2, 0, i, 2)
                step(i * 2 + 1, 1, i, 2)
            step(NC - 4, 0, NC // 2 - 2, 2)
            step(NC - 3, 1, NC // 2 - 2, 1)
            step(NC - 2, 0, NC // 2 - 1, 0)
            epilogue()


        @block.sync
        def _(sp):
            sp.dma_start(x_in[:], x_t[0]).then_inc(x_loaded, 16)
            sp.dma_start(raw_in.rearrange("p j c -> p (j c)").rearrange("p (k c) -> p k c", k=KD),
                         w_in.rearrange("(k p) c -> p k c", p=P)).then_inc(win_loaded, 16)
            sp.dma_start(tap_w[:], conv_w.rearrange("(j p) o t -> p j (o t)", p=P)).then_inc(w_loaded, 16)
            with nc.allow_non_contiguous_dma(reason="small transposed loads, once"):
                sp.dma_start(tap_b[:], conv_b.rearrange("(j p) -> p j", p=P)).then_inc(w_loaded, 16)
                sp.dma_start(b1_all[:], b1.rearrange("e (k p) -> p e k", p=P)).then_inc(w_loaded, 16)
            sp.dma_start(wb_raw[:], w_B.rearrange("(j p) s -> p j s", p=P)).then_inc(w_loaded, 16)
            for r in range(P // NST):
                sp.dma_start(raw_c[r * NST:(r + 1) * NST, :], w_C).then_inc(w_loaded, 16)
            sp.dma_start(raw_out.rearrange("p h c -> p (h c)").rearrange("p (j c) -> p j c", j=JD),
                         w_out.rearrange("(j p) c -> p j c", p=P)).then_inc(win_loaded, 16)
            sp.dma_start(x_mid[:, 0], x_t[0]).then_inc(res_loaded[0], 16)
            sp.wait_ge(norm1_ready, 1)
            sp.dma_start(x_in[:], x_t[1]).then_inc(x_loaded, 16)
            sp.dma_start(w_router[:], Wr.rearrange("(k p) e -> p k e", p=P)).then_inc(w_loaded, 16)
            sp.dma_start(b_router[:], br.rearrange("(o e) -> o e", o=1)).then_inc(w_loaded, 16)
            sp.dma_start(w1_all[:].rearrange("p e (k d) -> p e k d", k=KD),
                         W1.rearrange("e (k p) d -> p e k d", p=P)).then_inc(e_loaded, 16)
            sp.dma_start(w2_all[:].rearrange("p e (k d) -> p e k d", k=KD),
                         W2.rearrange("e (k p) d -> p e k d", p=P)).then_inc(e_loaded, 16)
            sp.dma_start(b2_all[:], b2.rearrange("(o e) d -> o e d", o=1).broadcast_to([P, E, D])).then_inc(w_loaded, 16)
            sp.dma_start(x_mid[:, 1], x_t[1]).then_inc(res_loaded[1], 16)

            def fetch(c):
                sp.wait_ge(norm1_ready, c)
                sp.dma_start(x_in[:], x_t[c]).then_inc(x_loaded, 16)

            def store(f, q):
                sp.wait_ge(done, f * 2 + 4)
                sp.dma_start(out_t[f], x_mid[:, q]).then_inc(stored[q], 16)

            def refill(c, q, seq):
                sp.wait_ge(stored[q], seq * 16)
                sp.dma_start(x_mid[:, q], x_t[c]).then_inc(res_loaded[q], 16)

            fetch(2)
            with sp.Fori(0, NC // 2 - 2) as i:
                fetch(i * 2 + 3)
                store(i * 2, 0)
                refill(i * 2 + 2, 0, i + 1)
                fetch(i * 2 + 4)
                store(i * 2 + 1, 1)
                refill(i * 2 + 3, 1, i + 1)
            fetch(NC - 1)
            store(NC - 4, 0)
            refill(NC - 2, 0, NC // 2 - 1)
            store(NC - 3, 1)
            refill(NC - 1, 1, NC // 2 - 1)
            store(NC - 2, 0)
            store(NC - 1, 1)
            for q in range(2):
                sp.wait_ge(stored[q], 16 * (NC // 2))

        @block.gpsimd
        def _(pool):
            nc.gpsimd.memset(minus_half[:], -0.5).then_inc(consts_set, 1)
            nc.gpsimd.memset(ident[:], 0.0).then_inc(consts_set, 1)
            nc.gpsimd.memset(decay[:], DECAY).then_inc(consts_set, 1)
            pool.wait_ge(consts_set, 3)
            nc.gpsimd.affine_select(out=ident[:], in_=ident[:], compare_op=ALU.not_equal, fill=1.0, base=0,
                                    pattern=[[-1, P]], channel_multiplier=1).then_inc(consts_set, 1)
            pool.wait_ge(consts_set, 4)

            def norm1(c):
                pool.wait_ge(stats1_ready, c + 1)
                nc.gpsimd.tensor_tensor(rstd1[:], var_eps1[:], minus_half[:], ALU.pow).then_inc(rstd1_set, 1)
                pool.wait_ge(rstd1_set, c + 1)
                pool.sem_inc(passed, 1)
                for n in range(TT):
                    ins = nc.gpsimd.tensor_scalar(normed[:, n, :], x_in[:, n, :], neg_mean[:, n:n + 1],
                                                  rstd1[:, n:n + 1], ALU.add, ALU.mult)
                ins.then_inc(norm1_ready, 1)

            def pow2(f, h):
                pool.wait_ge(stats2_ready, f * 2 + h + 1)
                n = slice(2 * h, 2 * h + 2)
                nc.gpsimd.tensor_tensor(rstd2[:, n], var_eps2[:, n], minus_half[:, n], ALU.pow).then_inc(rstd2_set, 1)

            def split_conv(a, js):
                for j in js:
                    pool.wait_ge(xc_hi_set, a * JD + j + 1)
                    nc.gpsimd.tensor_tensor(xc_lo[:, j, :], conv[:, j, 0:CH], xc_hi[:, j, :].bitcast(F32),
                                            ALU.subtract).then_inc(xc_lo_set, 1)

            def split_hidden(f):
                for j in range(JF):
                    pool.wait_ge(g_hi, f * JF + j + 1)
                    nc.gpsimd.tensor_tensor(hid_lo[:, j, :], hid[:, j % 2, :], hid_hi[:, j, :].bitcast(F32),
                                            ALU.subtract).then_inc(g_lo, 1)

            def add_b2(f, q):
                pool.wait_ge(b_sel, (f - q) * 2 + 4)
                pool.wait_ge(norm2_ready, f * 2 + 2)
                for n in range(TT):
                    ins = nc.gpsimd.tensor_tensor(x_mid[:, q, n, :], x_mid[:, q, n, :], b2_sel[:], ALU.add)
                ins.then_inc(b2_added, 1)

            def prologue():
                norm1(0)
                pool.wait_ge(turned1, KD)
                norm1(1)
                split_conv(0, range(JD))
                pool.wait_ge(turned1, 2 * KD)
                norm1(2)

            def step(f, q, seq, left):
                a = f + 1
                pow2(f, 0)
                split_conv(a, (0, 1))
                pow2(f, 1)
                split_conv(a, (2, 3))
                add_b2(f, q)
                split_hidden(f)
                if left == 2:
                    pool.wait_ge(turned2, f * KD + KD)
                    norm1(a + 2)

            def epilogue():
                f = NC - 1
                pow2(f, 0)
                pow2(f, 1)
                add_b2(f, 1)
                split_hidden(f)

            steps(pool, prologue, step, epilogue)

        @block.scalar
        def _(act):
            def hi(dst, src, scale=1.0):
                return nc.scalar.activation(dst, src, ACT.Copy, scale=scale)

            act.wait_ge(win_loaded, 32)
            hi(w_in_hi[:].rearrange("p k c -> p (k c)"), raw_in.rearrange("p j c -> p (j c)")).then_inc(w_hi_set, 1)
            hi(w_out_hi[:].rearrange("p k c -> p (k c)"), raw_out.rearrange("p h c -> p (h c)")).then_inc(w_hi_set, 1)
            act.wait_ge(w_loaded, 16 * NW)
            nc.scalar.activation(state[:, 0, :], raw_c, ACT.Copy, scale=GAIN).then_inc(w_hi_set, 1)
            act.wait_ge(w_hi_set, 3)
            hi(c_mix[:], state[:, 0, :]).then_inc(w_hi_set, 1)
            for r in range(REP):
                hi(b_mix[:, :, 2 * r * NST:(2 * r + 1) * NST], wb_raw[:]).then_inc(w_hi_set, 1)

            def turn1_hi(c, q):
                for k in range(KD):
                    act.wait_ge(turned1, c * KD + k + 1)
                    hi(xn1_hi[:, q, k, :], turn[k][:]).then_inc(t1_hi, 1)

            def turn2_hi(f):
                for k in range(KD):
                    act.wait_ge(turned2, f * KD + k + 1)
                    hi(xn2_hi[:, k, :], turn[k][:]).then_inc(t2_hi, 1)

            def first_token(seq):
                act.wait_ge(turned_first, seq + 1)
                for k in range(KD):
                    hi(first_tok[:, k:k + 1], turn[k][:, 0:1]).then_inc(first_set, 1)

            def first_taps(a):
                act.wait_ge(edge_set, a + 1)
                for j in range(JD):
                    act.wait_ge(xp_ready, a * JD + j + 1)
                    nc.scalar.activation(conv[:, j, HALO:HALO + CH], blk[j][:], ACT.Identity, bias=tap_b[:, j:j + 1],
                                         scale=tap_w[:, j, 0:1]).then_inc(tap_first, 1)

            def silu(a, j):
                act.wait_ge(tap_added, a * JD * HALO + (j // 2) * 2 * HALO + 2 * (HALO - 1) + j % 2 + 1)
                nc.scalar.activation(conv[:, j, 0:CH], conv[:, j, 0:CH], ACT.Silu).then_inc(silu_set, 1)

            def silu_hi(a, j):
                act.wait_ge(silu_set, a * JD + j + 1)
                hi(xc_hi[:, j, :], conv[:, j, 0:CH]).then_inc(xc_hi_set, 1)

            def gates(a, j):
                act.wait_ge(z_ready, a * JD + j + 1)
                nc.scalar.activation(gate[:, j, :], blk[j][:], ACT.Silu).then_inc(gate_set, 1)

            def choose_w(f, seq, e_regs, which):
                raw, his, scale = ((w1_all, w1_hi, 1.0), (w2_all, w2_hi, 1.0 / TOP_K))[which]
                for t, e in enumerate(e_regs):
                    hi(his[:, t, :], raw[:, bass.ds(e, 1), :].rearrange("p o c -> p (o c)"), scale).then_inc(e_hi, 1)

            def gelus(f):
                for j in range(JF):
                    act.wait_ge(up_ready, f * JF + j + 1)
                    if j >= 2:
                        act.wait_ge(g_lo, f * JF + j - 1)
                    nc.scalar.activation(hid[:, j % 2, :], blk[j][:], ACT.Gelu,
                                         bias=b1_sel[:, j // KD, j % KD:j % KD + 1]).then_inc(gelu_set, 1)
                    act.wait_ge(gelu_set, f * JF + j + 1)
                    hi(hid_hi[:, j, :], hid[:, j % 2, :]).then_inc(g_hi, 1)

            def state_hi(a, qa):
                act.wait_ge(scanned, a + 1)
                hi(state_mix[:], state[:, qa, :]).then_inc(h_hi, 1)

            def y_his(a):
                for j in range(JD):
                    act.wait_ge(y_set, a * JD + j + 1)
                    hi(y_hi[:, j, :], gate[:, j, :]).then_inc(y_hi_set, 1)

            def prologue():
                turn1_hi(0, 0)
                act.wait_ge(w_lo_set, 4 + REP)
                first_taps(0)
                turn1_hi(1, 1)
                for j in range(JD):
                    silu(0, j)
                    silu_hi(0, j)
                for j in range(JD):
                    gates(0, j)
                state_hi(0, 0)
                y_his(0)

            def step(f, q, seq, left):
                a, qa = f + 1, 1 - q
                first_taps(a)
                if left:
                    turn1_hi(a + 1, q)
                silu(a, 0)
                silu(a, 1)
                silu_hi(a, 0)
                silu_hi(a, 1)
                gates(a, 0)
                silu(a, 2)
                gates(a, 1)
                silu_hi(a, 2)
                silu(a, 3)
                gates(a, 2)
                silu_hi(a, 3)
                if q == 0:
                    first_token(seq)
                gates(a, 3)
                turn2_hi(f)
                if q == 0:
                    act.wait_ge(e_loaded, 32)
                    act.wait_ge(route_step, seq * 3 + 3)
                    act.sem_inc(passed, 1)
                    chosen = [nc.scalar.value_load(expert[0:1, t:t + 1], min_val=0, max_val=E - 1) for t in range(TOP_K)]
                    choose_w(f, seq, chosen, 0)
                state_hi(a, qa)
                if q == 0:
                    choose_w(f, seq, chosen, 1)
                    act.wait_ge(b_sel, seq * 4 + 1)
                gelus(f)
                y_his(a)

            def epilogue():
                turn2_hi(NC - 1)
                gelus(NC - 1)

            steps(act, prologue, step, epilogue)

        @block.vector
        def _(dve):
            def lo(dst, src, hi):
                return nc.vector.tensor_tensor(dst, src, hi.bitcast(F32), ALU.subtract)

            dve.sem_inc(done, 2)

            def stats1(c):
                dve.wait_ge(x_loaded, c * 16 + 16)
                for n in range(TT):
                    ins = nc.vector.bn_stats(stats1_t[:, n, :], x_in[:, n, :])
                ins.then_inc(stat1_step, 1)
                if not (isinstance(c, int) and c == 0):
                    dve.wait_ge(norm1_ready, c)
                dve.wait_ge(stat1_step, c * 2 + 1)
                dve.sem_inc(passed, 1)
                for n in range(TT):
                    ins = nc.vector.bn_aggr(mean_var1[:, n, :], stats1_t[:, n, :])
                ins.then_inc(stat1_step, 1)
                dve.wait_ge(stat1_step, c * 2 + 2)
                nc.vector.tensor_scalar(neg_mean[:], mean_var1[:, :, 0], -1.0, None, ALU.mult)
                nc.vector.tensor_scalar(var_eps1[:], mean_var1[:, :, 1], EPS, None, ALU.add).then_inc(stats1_ready, 1)

            def residual(f, q, seq, h):
                if h == 0:
                    dve.wait_ge(res_loaded[q], seq * 16 + 16)
                dve.wait_ge(mixed, f * 2 + h + 1)
                rows = x_mid[:, q, 2 * h:2 * h + 2, :].rearrange("p n d -> p (n d)")
                nc.vector.tensor_tensor(rows, tok[h][:], rows, ALU.add).then_inc(mid_set, 1)

            def stats2(f, q, h):
                dve.wait_ge(mid_set, f * 2 + h + 1)
                tiles = (2 * h, 2 * h + 1)
                for n in tiles:
                    ins = nc.vector.bn_stats(stats2_t[:, n, :], x_mid[:, q, n, :])
                ins.then_inc(stat2_step, 1)
                dve.wait_ge(stat2_step, f * 4 + 2 * h + 1)
                dve.sem_inc(passed, 1)
                for n in tiles:
                    ins = nc.vector.bn_aggr(mean_var2[:, n, :], stats2_t[:, n, :])
                ins.then_inc(stat2_step, 1)
                dve.wait_ge(stat2_step, f * 4 + 2 * h + 2)
                nc.vector.tensor_scalar(var_eps2[:, 2 * h:2 * h + 2], mean_var2[:, 2 * h:2 * h + 2, 1], EPS, None,
                                        ALU.add).then_inc(stats2_ready, 1)

            def norm2(f, q, h):
                dve.wait_ge(rstd2_set, f * 2 + h + 1)
                for n in (2 * h, 2 * h + 1):
                    ins = nc.vector.tensor_scalar(normed[:, n, :], x_mid[:, q, n, :], mean_var2[:, n, 0:1],
                                                  rstd2[:, n:n + 1], ALU.subtract, ALU.mult)
                ins.then_inc(norm2_ready, 1)

            def turn1_lo(c, q):
                for k in range(KD):
                    dve.wait_ge(t1_hi, c * KD + k + 1)
                    lo(xn1_lo[:, q, k, :], turn[k][:], xn1_hi[:, q, k, :]).then_inc(t1_lo, 1)

            def turn2_lo(f):
                for k in range(KD):
                    dve.wait_ge(t2_hi, f * KD + k + 1)
                    lo(xn2_lo[:, k, :], turn[k][:], xn2_hi[:, k, :]).then_inc(t2_lo, 1)

            def taps(a, pair):
                for t in range(1, TAPS):
                    for jj in range(2):
                        j = 2 * pair + jj
                        if t == 1:
                            dve.wait_ge(tap_first, a * JD + j + 1)
                        else:
                            dve.wait_ge(tap_added, a * JD * HALO + pair * 2 * HALO + (t - 2) * 2 + jj + 1)
                        cols = conv[:, j, HALO - t:HALO - t + CH]
                        nc.vector.scalar_tensor_tensor(cols, blk[j][:], tap_w[:, j, t:t + 1], cols, ALU.mult,
                                                       ALU.add).then_inc(tap_added, 1)

            def edge(c, opens):
                if opens:
                    src = tap_b[:].rearrange("p (j o) -> p j o", o=1).broadcast_to([P, JD, HALO])
                else:
                    src = conv[:, :, CH:CH + HALO]
                if not (isinstance(c, int) and c == 0):
                    dve.wait_ge(xc_lo_set, c * JD)
                nc.vector.tensor_copy(conv[:, :, 0:HALO], src).then_inc(edge_set, 1)

            def scan(a, qa):
                dve.wait_ge(u_ready, a + 1)
                start = 0.0 if qa == 0 else state[:, 0, CH - 1:CH]
                nc.vector.tensor_tensor_scan(state[:, qa, :], decay[:], tok[1][:], start, ALU.mult,
                                             ALU.add).then_inc(scanned, 1)

            def state_lo(a, qa):
                dve.wait_ge(h_hi, a + 1)
                lo(state_mix[P // 2:P, :], state[P // 2:P, qa, :], state_mix[P // 2:P, :]).then_inc(h_lo, 1)

            def ys(a):
                for j in range(JD):
                    dve.wait_ge(c_ready, a * JD + j + 1)
                    nc.vector.tensor_tensor(gate[:, j, :], blk[j][:], gate[:, j, :], ALU.mult).then_inc(y_set, 1)

            def ys_lo(a):
                for j in range(JD):
                    dve.wait_ge(y_hi_set, a * JD + j + 1)
                    lo(y_lo[:, j, :], gate[:, j, :], y_hi[:, j, :]).then_inc(y_lo_set, 1)

            def finish(f, q, h):
                dve.wait_ge(down_ready, f * 2 + h + 1)
                dve.wait_ge(b2_added, f + 1)
                rows = x_mid[:, q, 2 * h:2 * h + 2, :].rearrange("p n d -> p (n d)")
                nc.vector.tensor_tensor(rows, tok[h][:], rows, ALU.add).then_inc(done, 1)

            def route(seq):
                dve.wait_ge(scored, seq + 1)
                nc.vector.tensor_tensor(scores[:], tok[0][0:1, 0:E], b_router[:], ALU.add).then_inc(route_step, 1)
                dve.wait_ge(route_step, seq * 3 + 1)
                dve.sem_inc(passed, 1)
                nc.vector.max(best[:], scores[:]).then_inc(route_step, 1)
                dve.wait_ge(route_step, seq * 3 + 2)
                dve.sem_inc(passed, 1)
                nc.vector.max_index(expert[:], best[:], scores[:]).then_inc(route_step, 1)
                dve.wait_ge(route_step, seq * 3 + 3)
                dve.sem_inc(passed, 1)
                return [nc.vector.value_load(expert[0:1, t:t + 1], min_val=0, max_val=E - 1) for t in range(TOP_K)]

            def choose_w(seq, chosen, which):
                raw, his, los, scale = ((w1_all, w1_hi, w1_lo, 1.0), (w2_all, w2_hi, w2_lo, 1.0 / TOP_K))[which]
                for t, e in enumerate(chosen):
                    dve.wait_ge(e_hi, seq * 4 + which * TOP_K + t + 1)
                    nc.vector.scalar_tensor_tensor(
                        los[:, t, :], raw[:, bass.ds(e, 1), :].rearrange("p o c -> p (o c)"), scale,
                        his[:, t, :].bitcast(F32), ALU.mult, ALU.subtract).then_inc(e_lo, 1)

            def choose_b(seq, chosen):
                for t, e in enumerate(chosen):
                    ins = nc.vector.tensor_copy(b1_sel[:, t, :], b1_all[:, bass.ds(e, 1), :].rearrange("p o k -> p (o k)"))
                ins.then_inc(b_sel, 1)
                nc.vector.tensor_scalar(b2_half[:], b2_all[:, bass.ds(chosen[0], 1), :].rearrange("p o d -> p (o d)"),
                                        1.0 / TOP_K, None, ALU.mult).then_inc(b_sel, 1)
                dve.wait_ge(b_sel, seq * 4 + 2)
                nc.vector.scalar_tensor_tensor(
                    b2_sel[:], b2_all[:, bass.ds(chosen[1], 1), :].rearrange("p o d -> p (o d)"),
                    1.0 / TOP_K, b2_half[:], ALU.mult, ALU.add).then_inc(b_sel, 2)

            def prologue():
                stats1(0)
                dve.wait_ge(w_hi_set, 1)
                lo(w_in_lo[:].rearrange("p k c -> p (k c)"), raw_in.rearrange("p j c -> p (j c)"),
                   w_in_hi[:].rearrange("p k c -> p (k c)")).then_inc(w_lo_set, 1)
                turn1_lo(0, 0)
                dve.wait_ge(w_hi_set, 2)
                lo(w_out_lo[:].rearrange("p k c -> p (k c)"), raw_out.rearrange("p h c -> p (h c)"),
                   w_out_hi[:].rearrange("p k c -> p (k c)")).then_inc(w_lo_set, 1)
                dve.wait_ge(w_hi_set, 4 + REP)
                for r in range(REP):
                    lo(b_mix[:, :, (2 * r + 1) * NST:(2 * r + 2) * NST], wb_raw[:],
                       b_mix[:, :, 2 * r * NST:(2 * r + 1) * NST]).then_inc(w_lo_set, 1)
                for r in (P // 4, 3 * P // 4):
                    rows = slice(r, r + P // 4)
                    lo(c_mix[rows, :], state[rows, 0, :], c_mix[rows, :]).then_inc(w_lo_set, 1)
                edge(0, True)
                stats1(1)
                taps(0, 0)
                turn1_lo(1, 1)
                taps(0, 1)
                edge(1, False)
                dve.wait_ge(consts_set, 4)
                scan(0, 0)
                state_lo(0, 0)
                ys(0)
                stats1(2)
                ys_lo(0)

            def step(f, q, seq, left):
                a, qa = f + 1, 1 - q
                taps(a, 0)
                if left:
                    turn1_lo(a + 1, q)
                residual(f, q, seq, 0)
                stats2(f, q, 0)
                taps(a, 1)
                norm2(f, q, 0)
                residual(f, q, seq, 1)
                stats2(f, q, 1)
                norm2(f, q, 1)
                if q == 0:
                    dve.wait_ge(e_loaded, 32)
                    chosen = route(seq)
                turn2_lo(f)
                if q == 0:
                    choose_w(seq, chosen, 0)
                if left:
                    edge(a + 1, qa == 1)
                scan(a, qa)
                if q == 0:
                    choose_b(seq, chosen)
                state_lo(a, qa)
                if q == 0:
                    choose_w(seq, chosen, 1)
                if left == 2:
                    stats1(a + 2)
                finish(f, q, 0)
                ys(a)
                finish(f, q, 1)
                ys_lo(a)

            def epilogue():
                f = NC - 1
                for h in range(2):
                    residual(f, 1, NC // 2 - 1, h)
                    stats2(f, 1, h)
                norm2(f, 1, 0)
                norm2(f, 1, 1)
                turn2_lo(f)
                finish(f, 1, 0)
                finish(f, 1, 1)

            steps(dve, prologue, step, epilogue)

        @block.tensor
        def _(pe):
            mm = nc.tensor.matmul

            def turns(tiles, sem_out):
                for k in range(KD):
                    for t in tiles:
                        ins = nc.tensor.transpose(turn[k][:, t * P:(t + 1) * P], normed[:, t, k * P:(k + 1) * P],
                                                  ident[:])
                    if sem_out is not None:
                        ins.then_inc(sem_out, 1)
                return ins

            def turns1(c):
                pe.wait_ge(norm1_ready, c + 1)
                turns(range(TT), turned1)

            def project(j, whi, wlo, his, los, los_ready, c, sem_out):
                dst = blk[j][:]
                for k in range(KD):
                    mm(dst, whi(k), his(k), start=(k == 0), stop=False)
                    mm(dst, wlo(k), his(k), start=False, stop=False)
                for k in range(KD):
                    if los_ready is not None:
                        pe.wait_ge(los_ready, c * KD + k + 1)
                    ins = mm(dst, whi(k), los(k), start=False, stop=(k == KD - 1))
                ins.then_inc(sem_out, 1)

            def in_proj(a, qa, j, part, sem_out):
                cols = slice(part * DI + j * P, part * DI + (j + 1) * P)
                project(j, lambda k: w_in_hi[:, k, cols], lambda k: w_in_lo[:, k, cols],
                        lambda k: xn1_hi[:, qa, k, :], lambda k: xn1_lo[:, qa, k, :],
                        t1_lo if part == 0 and j == 0 else None, a, sem_out)

            def xp(a, qa):
                pe.wait_ge(t1_hi, a * KD + KD)
                for j in range(JD):
                    if not (isinstance(a, int) and a == 0):
                        pe.wait_ge(y_set, a * JD - JD + j + 1)
                    in_proj(a, qa, j, 0, xp_ready)

            def z(a, qa, j):
                pe.wait_ge(tap_added, a * JD * HALO + (j // 2) * 2 * HALO + 2 * (HALO - 1) + j % 2 + 1)
                in_proj(a, qa, j, 1, z_ready)

            def up(f, q, seq):
                pe.wait_ge(t2_hi, f * KD + KD)
                for j in range(JF):
                    if q == 0 and j % KD == 0:
                        pe.wait_ge(e_lo, seq * 4 + j // KD + 1)
                    if not (isinstance(f, int) and f == NC - 1):
                        pe.wait_ge(gate_set, f * JD + JD + j + 1)
                    t, m = j // KD, j % KD
                    project(j, lambda k: w1_hi[:, t, k * D + m * P:k * D + (m + 1) * P],
                            lambda k: w1_lo[:, t, k * D + m * P:k * D + (m + 1) * P],
                            lambda k: xn2_hi[:, k, :], lambda k: xn2_lo[:, k, :], t2_lo if j == 0 else None, f, up_ready)

            def tokens(h, j, last, his, los, whi, wlo):
                for n in range(2):
                    rows = slice((2 * h + n) * P, (2 * h + n + 1) * P)
                    dst = tok[h][:, n * D:(n + 1) * D]
                    mm(dst, his[:, j, rows], whi, start=(j == 0 and n == 0), stop=False, skip_group_check=True)
                    mm(dst, his[:, j, rows], wlo, start=False, stop=False, skip_group_check=True)
                    ins = mm(dst, los[:, j, rows], whi, start=False, stop=(last and n == 1), skip_group_check=True)
                return ins

            def down(f, h):
                for j in range(JF):
                    if h == 0:
                        pe.wait_ge(g_lo, f * JF + j + 1)
                    t, cols = j // KD, slice(j % KD * D, (j % KD + 1) * D)
                    ins = tokens(h, j, j == JF - 1, hid_hi, hid_lo, w2_hi[:, t, cols], w2_lo[:, t, cols])
                ins.then_inc(down_ready, 1)

            def out_proj(f, h):
                pe.wait_ge(done, f * 2 + h + 1)
                for j in range(JD):
                    if h == 0:
                        pe.wait_ge(y_lo_set, f * JD + j + 1)
                    ins = tokens(h, j, j == JD - 1, y_hi, y_lo, w_out_hi[:, j, :], w_out_lo[:, j, :])
                ins.then_inc(mixed, 1)

            def state_in(a):
                for part, ready in ((xc_hi, xc_hi_set), (xc_lo, xc_lo_set)):
                    for j in range(JD):
                        pe.wait_ge(ready, a * JD + j + 1)
                        ins = mm(tok[1][:], b_mix[:, j, :], part[:, j, :], start=(part is xc_hi and j == 0),
                                 stop=(part is xc_lo and j == JD - 1))
                ins.then_inc(u_ready, 1)

            def state_out(a):
                pe.wait_ge(h_lo, a + 1)
                for j in range(JD):
                    mm(blk[j][:], c_mix[:, j * P:(j + 1) * P], state_mix[:], start=True,
                       stop=True).then_inc(c_ready, 1)

            def prologue():
                pe.wait_ge(consts_set, 4)
                turns1(0)
                pe.wait_ge(w_lo_set, 1)
                xp(0, 0)
                turns1(1)
                for j in range(JD):
                    z(0, 0, j)
                pe.wait_ge(w_lo_set, 4 + REP)
                state_in(0)
                pe.wait_ge(gate_set, JD)
                state_out(0)

            def step(f, q, seq, left):
                a, qa = f + 1, 1 - q
                xp(a, qa)
                if left:
                    turns1(a + 1)
                out_proj(f, 0)
                out_proj(f, 1)
                for j in range(JD - 1):
                    z(a, qa, j)
                if left:
                    pe.wait_ge(t1_lo, a * KD + 2 * KD)
                pe.wait_ge(norm2_ready, f * 2 + 1)
                ins = turns(range(2), None)
                if q == 0:
                    ins.then_inc(turned_first, 1)
                z(a, qa, JD - 1)
                if q == 0:
                    pe.wait_ge(first_set, seq * KD + KD)
                pe.wait_ge(norm2_ready, f * 2 + 2)
                turns(range(2, TT), turned2)
                if q == 0:
                    for k in range(KD):
                        ins = mm(tok[0][0:1, 0:E], first_tok[:, k:k + 1], w_router[:, k, :], start=(k == 0),
                                 stop=(k == KD - 1))
                    ins.then_inc(scored, 1)
                state_in(a)
                up(f, q, seq)
                if q == 0:
                    pe.wait_ge(e_lo, seq * 4 + 4)
                down(f, 0)
                state_out(a)
                down(f, 1)

            def epilogue():
                f = NC - 1
                out_proj(f, 0)
                out_proj(f, 1)
                pe.wait_ge(norm2_ready, 2 * NC)
                turns(range(TT), turned2)
                pe.wait_ge(y_set, NC * JD)
                up(f, 1, None)
                down(f, 0)
                down(f, 1)

            steps(pe, prologue, step, epilogue)


_INS = ["L0_attn_x", "L0_attn_w_in", "L0_attn_conv_w", "L0_attn_conv_b", "L0_attn_w_B", "L0_attn_w_C",
        "L0_attn_w_out", "L0_ffn_Wr", "L0_ffn_br", "L0_ffn_W1", "L0_ffn_b1", "L0_ffn_W2", "L0_ffn_b2"]


def kernel(**inputs):
    import numpy as _np
    import concourse.bacc as _bacc
    from concourse import mybir as _mybir
    from concourse.bass_utils import run_bass_kernel_spmd as _run

    nc = _bacc.Bacc("TRN2", target_bir_lowering=False, num_devices=1)
    arrays, args = {}, []
    for name in _INS:
        a = _np.ascontiguousarray(inputs[name])
        arrays[f"in_{name}"] = a
        args.append(nc.dram_tensor(f"in_{name}", a.shape, _mybir.dt.from_np(a.dtype), kind="ExternalInput").ap())
    shape = inputs["L0_attn_x"].shape
    args.append(nc.dram_tensor("out_0", shape, F32, kind="ExternalOutput").ap())
    build_block(nc, *args)
    r = _run(nc, [arrays], core_ids=[0])
    return r.results[0]["out_0"]
```

```python
from contextlib import ExitStack

import concourse.bass as bass
from concourse import mybir

ALU = mybir.AluOpType
ACT = mybir.ActivationFunctionType
F32 = mybir.dt.float32
F32R = mybir.dt.float32r
U32 = mybir.dt.uint32

P = 128
DECAY, GAIN = 0.9, 0.1
EPS = 1e-5
TOP_K = 2


def build_block(nc, x, w_in, conv_w, conv_b, w_B, w_C, w_out, Wr, br, W1, b1, W2, b2, out):
    B, S, D = x.shape
    DI = w_out.shape[0]
    NST = w_B.shape[1]
    TAPS = conv_w.shape[2]
    E = Wr.shape[1]
    CH = 512
    PER = S // CH
    NC = B * PER
    TT = CH // P
    KD = D // P
    JD = DI // P
    JF = TOP_K * KD
    HALO = TAPS - 1
    REP = P // (2 * NST)
    assert PER == 2 and TT == 4 and KD == 2 and JD == 4 and JF == 4 and NST == 16 and E == 8

    x_t = x.rearrange("b s d -> (b s) d").rearrange("(c n p) d -> c p n d", p=P, n=TT)
    out_t = out.rearrange("b s d -> (b s) d").rearrange("(c n p) d -> c p n d", p=P, n=TT)

    with ExitStack() as ctx:
        def sb(name, shape, dt=F32):
            return ctx.enter_context(nc.sbuf_tensor(name, shape, dt))

        def sem(name):
            return ctx.enter_context(nc.semaphore(name))

        ident = sb("ident", [P, P])
        decay = sb("decay", [P, CH])
        w_in_hi, w_in_lo = sb("w_in_hi", [P, KD, 2 * DI], F32R), sb("w_in_lo", [P, KD, 2 * DI], F32R)
        w_out_hi, w_out_lo = sb("w_out_hi", [P, JD, D], F32R), sb("w_out_lo", [P, JD, D], F32R)
        b_mix = sb("b_mix", [P, JD, P], F32R)
        c_mix = sb("c_mix", [P, DI], F32R)
        wb_raw = sb("wb_raw", [P, JD, NST])
        tap_w = sb("tap_w", [P, JD, TAPS])
        tap_b = sb("tap_b", [P, JD])
        w_router = sb("w_router", [P, KD, E])
        b_router = sb("b_router", [1, E])
        w1_all, w2_all = sb("w1_all", [P, E, KD * D]), sb("w2_all", [P, E, KD * D])
        b1_all = sb("b1_all", [P, E, KD])
        b2_all = sb("b2_all", [P, E, D])
        w1_hi, w1_lo = sb("w1_hi", [P, TOP_K, KD * D], F32R), sb("w1_lo", [P, TOP_K, KD * D], F32R)
        w2_hi, w2_lo = sb("w2_hi", [P, TOP_K, KD * D], F32R), sb("w2_lo", [P, TOP_K, KD * D], F32R)
        b1_sel = sb("b1_sel", [P, TOP_K, KD])
        b2_sum, b2_sel = sb("b2_sum", [P, D]), sb("b2_sel", [P, D])
        scores = sb("scores", [1, E])
        best = sb("best", [1, 8])
        expert = sb("expert", [1, 8], U32)

        x_in = sb("x_in", [P, TT, D])
        x_mid = sb("x_mid", [P, 2, TT, D])
        normed = sb("normed", [P, TT, D])
        stats1_t, stats2_t = sb("stats1_t", [P, TT, 6]), sb("stats2_t", [P, TT, 6])
        mean_var1, mean_var2 = sb("mean_var1", [P, TT, 2]), sb("mean_var2", [P, TT, 2])
        var_eps1, var_eps2 = sb("var_eps1", [P, TT]), sb("var_eps2", [P, TT])
        rstd1, rstd2 = sb("rstd1", [P, TT]), sb("rstd2", [P, TT])
        neg_mean = sb("neg_mean", [P, TT])
        minus_half = sb("minus_half", [P, TT])
        unused = sb("unused", [1, 1])
        xn1_hi, xn1_lo = sb("xn1_hi", [P, KD, CH], F32R), sb("xn1_lo", [P, KD, CH], F32R)
        xn2_hi, xn2_lo = sb("xn2_hi", [P, KD, CH], F32R), sb("xn2_lo", [P, KD, CH], F32R)
        first_tok = sb("first_tok", [P, KD])
        conv = sb("conv", [P, JD, CH + HALO])
        xc_hi, xc_lo = sb("xc_hi", [P, JD, CH], F32R), sb("xc_lo", [P, JD, CH], F32R)
        gate = sb("gate", [P, JD, CH])
        y_hi, y_lo = sb("y_hi", [P, JD, CH], F32R), sb("y_lo", [P, JD, CH], F32R)
        state = sb("state", [P, 2, CH])
        state_mix = sb("state_mix", [P, CH], F32R)
        hid = sb("hid", [P, JF, CH])
        hid_hi, hid_lo = sb("hid_hi", [P, JF, CH], F32R), sb("hid_lo", [P, JF, CH], F32R)

        turn = [ctx.enter_context(nc.psum_tensor(f"turn{k}", [P, CH], F32)) for k in range(KD)]
        tok = [ctx.enter_context(nc.psum_tensor(f"tok{h}", [P, CH], F32)) for h in range(2)]
        blk = [ctx.enter_context(nc.psum_tensor(f"blk{j}", [P, CH], F32)) for j in range(JD)]

        win_loaded = [sem("win_loaded0"), sem("win_loaded1")]
        wout_loaded = sem("wout_loaded")
        taps_loaded = sem("taps_loaded")
        mix_loaded = sem("mix_loaded")
        late_loaded = sem("late_loaded")
        e_loaded = sem("e_loaded")
        x_loaded = sem("x_loaded")
        res_loaded = [sem("res_loaded0"), sem("res_loaded1")]
        consts_set = sem("consts_set")
        w_hi_set = sem("w_hi_set")
        w_lo_set = sem("w_lo_set")
        z_out_lo_set = sem("z_out_lo_set")
        stat1_step, stat2_step = sem("stat1_step"), sem("stat2_step")
        stats1_ready = sem("stats1_ready")
        stats2_ready = sem("stats2_ready")
        rstd1_set, rstd2_set = sem("rstd1_set"), sem("rstd2_set")
        norm1_ready = sem("norm1_ready")
        norm2_ready = sem("norm2_ready")
        turned1, turned2 = sem("turned1"), sem("turned2")
        turned_first = sem("turned_first")
        t1_hi, t1_lo = sem("t1_hi"), sem("t1_lo")
        t2_hi, t2_lo = sem("t2_hi"), sem("t2_lo")
        xp_ready = sem("xp_ready")
        tap_first = sem("tap_first")
        edge_set = sem("edge_set")
        tap_added = sem("tap_added")
        silu_set = sem("silu_set")
        xc_hi_set, xc_lo_set = sem("xc_hi_set"), sem("xc_lo_set")
        z_ready = sem("z_ready")
        gate_set = sem("gate_set")
        u_ready, scanned = sem("u_ready"), sem("scanned")
        h_hi, h_lo = sem("h_hi"), sem("h_lo")
        c_ready = sem("c_ready")
        y_set = sem("y_set")
        y_hi_set, y_lo_set = sem("y_hi_set"), sem("y_lo_set")
        mixed = sem("mixed")
        mid_set = sem("mid_set")
        b2_added = sem("b2_added")
        first_set = sem("first_set")
        scored = sem("scored")
        route_step = sem("route_step")
        w1_hi_set, w1_lo_set = sem("w1_hi_set"), sem("w1_lo_set")
        w2_hi_set, w2_lo_set = sem("w2_hi_set"), sem("w2_lo_set")
        b1_set = sem("b1_set")
        b2_set = sem("b2_set")
        up_ready = sem("up_ready")
        gelu_set = sem("gelu_set")
        g_hi = sem("g_hi")
        g_lo = sem("g_lo")
        down_ready = sem("down_ready")
        done = sem("done")
        stored = [sem("stored0"), sem("stored1")]
        half_turned = sem("half_turned")
        half_t2_hi, half_t2_lo = sem("half_t2_hi"), sem("half_t2_lo")
        half_up = sem("half_up")
        half_gelu, half_g_hi = sem("half_gelu"), sem("half_g_hi")
        half_g_lo = sem("half_g_lo")
        passed = sem("passed")

        raw_in = gate[:].rearrange("p j c -> p (j c)").rearrange("p (k c) -> p k c", k=KD)
        raw_out = hid[:, 0:JD * D // CH, :].rearrange("p h c -> p (h c)").rearrange("p (j c) -> p j c", j=JD)
        raw_c = hid[:, JF - 1, :]

        HT = CH // 2

        def half_cols(h):
            return slice(h * HT, (h + 1) * HT)

        def half_turn(h):
            return turn[h][:].rearrange("p (k t) -> p k t", k=KD)

        def half_blk(h, j):
            return blk[2 * h + j // 2][:, j % 2 * HT:(j % 2 + 1) * HT]

        block = ctx.enter_context(nc.Block())

        def steps(eng, prologue, step, epilogue):
            prologue()
            with eng.Fori(0, NC // 2 - 1) as i:
                step(i * 2, 0, i, True)
                step(i * 2 + 1, 1, i, True)
            step(NC - 2, 0, NC // 2 - 1, False)
            epilogue()


        @block.sync
        def _(sp):
            sp.dma_start(x_in[:], x_t[0]).then_inc(x_loaded, 16)
            z_cols = slice(DI, 2 * DI)
            sp.dma_start(raw_in[:, :, z_cols], w_in[:, z_cols].rearrange("(k p) c -> p k c", p=P)).then_inc(win_loaded[1], 16)
            sp.dma_start(raw_out, w_out.rearrange("(j p) c -> p j c", p=P)).then_inc(wout_loaded, 16)
            sp.wait_ge(norm1_ready, 1)
            sp.dma_start(x_in[:], x_t[1]).then_inc(x_loaded, 16)
            sp.dma_start(x_mid[:, 0], x_t[0]).then_inc(res_loaded[0], 16)
            sp.dma_start(x_mid[:, 1], x_t[1]).then_inc(res_loaded[1], 16)
            sp.dma_start(w_router[:], Wr.rearrange("(k p) e -> p k e", p=P)).then_inc(late_loaded, 16)
            sp.dma_start(b_router[:], br.rearrange("(o e) -> o e", o=1)).then_inc(late_loaded, 16)
            with nc.allow_non_contiguous_dma(reason="a small transposed load, once"):
                sp.dma_start(b1_all[:], b1.rearrange("e (k p) -> p e k", p=P)).then_inc(late_loaded, 16)
            sp.dma_start(w1_all[:].rearrange("p e (k d) -> p e k d", k=KD),
                         W1.rearrange("e (k p) d -> p e k d", p=P)).then_inc(e_loaded, 16)
            sp.dma_start(w2_all[:].rearrange("p e (k d) -> p e k d", k=KD),
                         W2.rearrange("e (k p) d -> p e k d", p=P)).then_inc(e_loaded, 16)
            sp.dma_start(b2_all[:], b2.rearrange("(o e) d -> o e d", o=1).broadcast_to([P, E, D])).then_inc(e_loaded, 16)

            def fetch(c):
                sp.wait_ge(norm1_ready, c)
                sp.dma_start(x_in[:], x_t[c]).then_inc(x_loaded, 16)

            def store(f, q):
                sp.wait_ge(done, f * 2 + 4)
                sp.dma_start(out_t[f], x_mid[:, q]).then_inc(stored[q], 16)

            def refill(c, q, seq):
                sp.wait_ge(stored[q], seq * 16)
                sp.dma_start(x_mid[:, q], x_t[c]).then_inc(res_loaded[q], 16)

            def step(f, q, seq, ahead):
                if ahead:
                    fetch(f + 3)
                store(f, q)
                refill(f + 2, q, seq + 1)

            fetch(2)
            with sp.Fori(0, NC // 2 - 2) as i:
                step(i * 2, 0, i, True)
                step(i * 2 + 1, 1, i, True)
            step(NC - 4, 0, NC // 2 - 2, True)
            step(NC - 3, 1, NC // 2 - 2, False)
            store(NC - 2, 0)
            for h in range(2):
                sp.wait_ge(done, NC * 2 + h + 1)
                sp.dma_start(out_t[NC - 1][:, 2 * h:2 * h + 2, :], x_mid[:, 1, 2 * h:2 * h + 2, :]).then_inc(stored[1], 16)
            sp.wait_ge(stored[0], 16 * (NC // 2))
            sp.wait_ge(stored[1], 16 * (NC // 2 + 1))

        @block.gpsimd
        def _(pool):
            nc.gpsimd.memset(minus_half[:], -0.5).then_inc(consts_set, 1)
            nc.gpsimd.memset(ident[:], 0.0).then_inc(consts_set, 1)
            nc.gpsimd.memset(decay[:], DECAY).then_inc(consts_set, 1)
            pool.wait_ge(consts_set, 3)
            nc.gpsimd.affine_select(out=ident[:], in_=ident[:], compare_op=ALU.not_equal, fill=1.0, base=0,
                                    pattern=[[-1, P]], channel_multiplier=1).then_inc(consts_set, 1)
            pool.wait_ge(consts_set, 4)

            def pow1(c):
                pool.wait_ge(stats1_ready, c + 1)
                nc.gpsimd.tensor_tensor(rstd1[:], var_eps1[:], minus_half[:], ALU.pow).then_inc(rstd1_set, 1)

            def norm1(c):
                pool.wait_ge(rstd1_set, c + 1)
                pool.sem_inc(passed, 1)
                for n in range(TT):
                    ins = nc.gpsimd.tensor_scalar(normed[:, n, :], x_in[:, n, :], neg_mean[:, n:n + 1],
                                                  rstd1[:, n:n + 1], ALU.add, ALU.mult)
                ins.then_inc(norm1_ready, 1)

            def pow2(f, h):
                pool.wait_ge(stats2_ready, f * 2 + h + 1)
                n = slice(2 * h, 2 * h + 2)
                nc.gpsimd.tensor_tensor(rstd2[:, n], var_eps2[:, n], minus_half[:, n], ALU.pow).then_inc(rstd2_set, 1)

            def split_conv(a, js):
                for j in js:
                    pool.wait_ge(xc_hi_set, a * JD + j + 1)
                    nc.gpsimd.tensor_tensor(xc_lo[:, j, :], conv[:, j, 0:CH], xc_hi[:, j, :].bitcast(F32),
                                            ALU.subtract).then_inc(xc_lo_set, 1)

            def choose_w2(seq):
                pool.wait_ge(e_loaded, 48)
                pool.wait_ge(route_step, seq * 3 + 3)
                pool.sem_inc(passed, 1)
                chosen = [nc.gpsimd.value_load(expert[0:1, t:t + 1], min_val=0, max_val=E - 1) for t in range(TOP_K)]
                for t in range(TOP_K):
                    raw = w2_all[:, bass.ds(chosen[t], 1), :].rearrange("p o c -> p (o c)")
                    nc.gpsimd.tensor_copy(w2_hi[:, t, :], raw).then_inc(w2_hi_set, 1)
                    pool.wait_ge(w2_hi_set, seq * TOP_K + t + 1)
                    pool.sem_inc(passed, 1)
                    nc.gpsimd.tensor_tensor(w2_lo[:, t, :], raw, w2_hi[:, t, :].bitcast(F32),
                                            ALU.subtract).then_inc(w2_lo_set, 1)
                return chosen

            def choose_b2(seq, chosen):
                rows = [b2_all[:, bass.ds(e, 1), :].rearrange("p o d -> p (o d)") for e in chosen]
                nc.gpsimd.tensor_tensor(b2_sum[:], rows[0], rows[1], ALU.add).then_inc(b2_set, 1)
                pool.wait_ge(b2_set, seq * 2 + 1)
                pool.sem_inc(passed, 1)
                nc.gpsimd.tensor_scalar(b2_sel[:], b2_sum[:], 1.0 / TOP_K, None, ALU.mult).then_inc(b2_set, 1)

            def split_y(a):
                for j in range(JD):
                    pool.wait_ge(y_hi_set, a * JD + j + 1)
                    nc.gpsimd.tensor_tensor(y_lo[:, j, :], gate[:, j, :], y_hi[:, j, :].bitcast(F32),
                                            ALU.subtract).then_inc(y_lo_set, 1)

            def add_b2(f, q, seq):
                if q == 0:
                    pool.wait_ge(b2_set, seq * 2 + 2)
                pool.wait_ge(norm2_ready, f * 2 + 2)
                for n in range(TT):
                    ins = nc.gpsimd.tensor_tensor(x_mid[:, q, n, :], x_mid[:, q, n, :], b2_sel[:], ALU.add)
                ins.then_inc(b2_added, 1)

            def prologue():
                def weights_lo(dst, src, his):
                    nc.gpsimd.tensor_tensor(dst, src, his.bitcast(F32), ALU.subtract).then_inc(z_out_lo_set, 1)

                pow1(0)
                norm1(0)
                pool.wait_ge(w_hi_set, 2)
                weights_lo(w_in_lo[:, :, DI:], raw_in[:, :, DI:], w_in_hi[:, :, DI:])
                pow1(1)
                pool.wait_ge(turned1, KD)
                norm1(1)
                pool.wait_ge(w_hi_set, 5 + REP)
                weights_lo(w_out_lo[:], raw_out, w_out_hi[:])
                split_conv(0, range(JD))
                split_y(0)

            def step(f, q, seq, more):
                a = f + 1
                split_conv(a, (0, 1))
                pow2(f, 0)
                split_conv(a, (2,))
                pow2(f, 1)
                split_conv(a, (3,))
                if q == 0:
                    chosen = choose_w2(seq)
                else:
                    add_b2(f, q, seq)
                if more:
                    pow1(a + 1)
                    pool.wait_ge(turned2, f * KD + KD)
                    norm1(a + 1)
                if q == 0:
                    choose_b2(seq, chosen)
                    add_b2(f, q, seq)
                if more:
                    split_y(a)

            def epilogue():
                f = NC - 1
                pow2(f, 0)
                pow2(f, 1)
                add_b2(f, 1, None)

            steps(pool, prologue, step, epilogue)

        @block.scalar
        def _(act):
            def hi(dst, src, scale=1.0):
                return nc.scalar.activation(dst, src, ACT.Copy, scale=scale)

            in_cols = [slice(part * DI, (part + 1) * DI) for part in range(2)]
            act.dma_start(raw_in[:, :, in_cols[0]],
                          w_in[:, in_cols[0]].rearrange("(k p) c -> p k c", p=P)).then_inc(win_loaded[0], 16)
            act.dma_start(tap_w[:], conv_w.rearrange("(j p) o t -> p j (o t)", p=P)).then_inc(taps_loaded, 16)
            with nc.allow_non_contiguous_dma(reason="a small transposed load, once"):
                act.dma_start(tap_b[:], conv_b.rearrange("(j p) -> p j", p=P)).then_inc(taps_loaded, 16)
            act.dma_start(wb_raw[:], w_B.rearrange("(j p) s -> p j s", p=P)).then_inc(mix_loaded, 16)
            for r in range(P // NST):
                act.dma_start(raw_c[r * NST:(r + 1) * NST, :], w_C).then_inc(mix_loaded, 16)
            for part, cols in enumerate(in_cols):
                act.wait_ge(win_loaded[part], 16)
                hi(w_in_hi[:, :, cols], raw_in[:, :, cols]).then_inc(w_hi_set, 1)

            def mix_hi():
                act.wait_ge(mix_loaded, 16 * (1 + P // NST))
                hi(state[:, 0, :], raw_c, GAIN).then_inc(w_hi_set, 1)
                for r in range(REP):
                    hi(b_mix[:, :, 2 * r * NST:(2 * r + 1) * NST], wb_raw[:]).then_inc(w_hi_set, 1)
                act.wait_ge(w_hi_set, 3 + REP)
                hi(c_mix[:], state[:, 0, :]).then_inc(w_hi_set, 1)

            def turn1_hi(c):
                for k in range(KD):
                    act.wait_ge(turned1, c * KD + k + 1)
                    hi(xn1_hi[:, k, :], turn[k][:]).then_inc(t1_hi, 1)

            def turn2_hi(f):
                for k in range(KD):
                    act.wait_ge(turned2, f * KD + k + 1)
                    hi(xn2_hi[:, k, :], turn[k][:]).then_inc(t2_hi, 1)

            def first_token(seq):
                act.wait_ge(turned_first, seq + 1)
                for k in range(KD):
                    hi(first_tok[:, k:k + 1], turn[k][:, 0:1]).then_inc(first_set, 1)

            def first_taps(a):
                act.wait_ge(edge_set, a + 1)
                for j in range(JD):
                    act.wait_ge(xp_ready, a * JD + j + 1)
                    nc.scalar.activation(conv[:, j, HALO:HALO + CH], blk[j][:], ACT.Identity, bias=tap_b[:, j:j + 1],
                                         scale=tap_w[:, j, 0:1]).then_inc(tap_first, 1)

            def silu(a, j):
                act.wait_ge(tap_added, a * JD * HALO + (j // 2) * 2 * HALO + 2 * (HALO - 1) + j % 2 + 1)
                nc.scalar.activation(conv[:, j, 0:CH], conv[:, j, 0:CH], ACT.Silu).then_inc(silu_set, 1)

            def silu_hi(a, j):
                act.wait_ge(silu_set, a * JD + j + 1)
                hi(xc_hi[:, j, :], conv[:, j, 0:CH]).then_inc(xc_hi_set, 1)

            def gates(a, j):
                act.wait_ge(z_ready, a * JD + j + 1)
                nc.scalar.activation(gate[:, j, :], blk[j][:], ACT.Silu).then_inc(gate_set, 1)

            def warm(func):
                nc.scalar.activation(unused[:], minus_half[0:1, 0:1], func)

            def choose_w1(t):
                e = nc.scalar.value_load(expert[0:1, t:t + 1], min_val=0, max_val=E - 1)
                hi(w1_hi[:, t, :], w1_all[:, bass.ds(e, 1), :].rearrange("p o c -> p (o c)")).then_inc(w1_hi_set, 1)

            def gelus(f):
                for j in range(JF + 1):
                    if j < JF:
                        act.wait_ge(up_ready, f * JF + j + 1)
                        nc.scalar.activation(hid[:, j, :], blk[j][:], ACT.Gelu,
                                             bias=b1_sel[:, j // KD, j % KD:j % KD + 1]).then_inc(gelu_set, 1)
                    if j > 0:
                        act.wait_ge(gelu_set, f * JF + j)
                        hi(hid_hi[:, j - 1, :], hid[:, j - 1, :]).then_inc(g_hi, 1)

            def state_hi(a, qa):
                act.wait_ge(scanned, a + 1)
                hi(state_mix[:], state[:, qa, :]).then_inc(h_hi, 1)

            def y_his(a):
                for j in range(JD):
                    act.wait_ge(y_set, a * JD + j + 1)
                    hi(y_hi[:, j, :], gate[:, j, :]).then_inc(y_hi_set, 1)

            def prologue():
                turn1_hi(0)
                mix_hi()
                act.wait_ge(wout_loaded, 16)
                hi(w_out_hi[:], raw_out).then_inc(w_hi_set, 1)
                act.wait_ge(consts_set, 1)
                act.wait_ge(taps_loaded, 32)
                first_taps(0)
                warm(ACT.Silu)
                for j in range(JD):
                    silu(0, j)
                    silu_hi(0, j)
                act.wait_ge(w_lo_set, 1)
                act.wait_ge(z_out_lo_set, 1)
                for j in range(JD):
                    gates(0, j)
                turn1_hi(1)
                state_hi(0, 0)
                y_his(0)

            def step(f, q, seq, more):
                a, qa = f + 1, 1 - q
                first_taps(a)
                silu(a, 0)
                silu(a, 1)
                silu_hi(a, 0)
                silu_hi(a, 1)
                gates(a, 0)
                silu(a, 2)
                silu(a, 3)
                silu_hi(a, 2)
                if q == 0:
                    first_token(seq)
                silu_hi(a, 3)
                gates(a, 1)
                gates(a, 2)
                if q == 0:
                    act.wait_ge(e_loaded, 48)
                    act.wait_ge(route_step, seq * 3 + 3)
                    act.sem_inc(passed, 1)
                    choose_w1(0)
                gates(a, 3)
                turn2_hi(f)
                if q == 0:
                    choose_w1(1)
                warm(ACT.Gelu)
                state_hi(a, qa)
                if q == 0:
                    act.wait_ge(b1_set, seq + 1)
                gelus(f)
                y_his(a)
                if more:
                    turn1_hi(a + 1)
                    warm(ACT.Silu)

            def epilogue():
                def turn2_half(h):
                    act.wait_ge(half_turned, h + 1)
                    hi(xn2_hi[:, :, half_cols(h)], half_turn(h)).then_inc(half_t2_hi, 1)

                def gelu_pair(h, first):
                    for j in (first, first + 1):
                        act.wait_ge(half_up, h * JF + first + 2)
                        nc.scalar.activation(hid[:, j, half_cols(h)], half_blk(h, j), ACT.Gelu,
                                             bias=b1_sel[:, j // KD, j % KD:j % KD + 1]).then_inc(half_gelu, 1)
                    for j in (first, first + 1):
                        act.wait_ge(half_gelu, h * JF + j + 1)
                        hi(hid_hi[:, j, half_cols(h)], hid[:, j, half_cols(h)]).then_inc(half_g_hi, 1)

                turn2_half(0)
                gelu_pair(0, 0)
                turn2_half(1)
                gelu_pair(0, 2)
                gelu_pair(1, 0)
                gelu_pair(1, 2)

            steps(act, prologue, step, epilogue)

        @block.vector
        def _(dve):
            def lo(dst, src, hi):
                return nc.vector.tensor_tensor(dst, src, hi.bitcast(F32), ALU.subtract)

            dve.sem_inc(done, 2)

            def stats1(c):
                dve.wait_ge(x_loaded, c * 16 + 16)
                for n in range(TT):
                    ins = nc.vector.bn_stats(stats1_t[:, n, :], x_in[:, n, :])
                ins.then_inc(stat1_step, 1)
                if not (isinstance(c, int) and c == 0):
                    dve.wait_ge(norm1_ready, c)
                dve.wait_ge(stat1_step, c * 2 + 1)
                dve.sem_inc(passed, 1)
                for n in range(TT):
                    ins = nc.vector.bn_aggr(mean_var1[:, n, :], stats1_t[:, n, :])
                ins.then_inc(stat1_step, 1)
                dve.wait_ge(stat1_step, c * 2 + 2)
                nc.vector.tensor_scalar(neg_mean[:], mean_var1[:, :, 0], -1.0, None, ALU.mult)
                nc.vector.tensor_scalar(var_eps1[:], mean_var1[:, :, 1], EPS, None, ALU.add).then_inc(stats1_ready, 1)

            def residual(f, q, seq, h):
                if h == 0:
                    dve.wait_ge(res_loaded[q], seq * 16 + 16)
                dve.wait_ge(mixed, f * 2 + h + 1)
                rows = x_mid[:, q, 2 * h:2 * h + 2, :].rearrange("p n d -> p (n d)")
                nc.vector.tensor_tensor(rows, tok[h][:], rows, ALU.add).then_inc(mid_set, 1)

            def stats2(f, q, h, between=(None, None)):
                dve.wait_ge(mid_set, f * 2 + h + 1)
                tiles = (2 * h, 2 * h + 1)
                for n in tiles:
                    ins = nc.vector.bn_stats(stats2_t[:, n, :], x_mid[:, q, n, :])
                ins.then_inc(stat2_step, 1)
                if between[0]:
                    between[0]()
                dve.wait_ge(stat2_step, f * 4 + 2 * h + 1)
                dve.sem_inc(passed, 1)
                for n in tiles:
                    ins = nc.vector.bn_aggr(mean_var2[:, n, :], stats2_t[:, n, :])
                ins.then_inc(stat2_step, 1)
                if between[1]:
                    between[1]()
                dve.wait_ge(stat2_step, f * 4 + 2 * h + 2)
                nc.vector.tensor_scalar(var_eps2[:, 2 * h:2 * h + 2], mean_var2[:, 2 * h:2 * h + 2, 1], EPS, None,
                                        ALU.add).then_inc(stats2_ready, 1)

            def norm2(f, q, h):
                dve.wait_ge(rstd2_set, f * 2 + h + 1)
                for n in (2 * h, 2 * h + 1):
                    ins = nc.vector.tensor_scalar(normed[:, n, :], x_mid[:, q, n, :], mean_var2[:, n, 0:1],
                                                  rstd2[:, n:n + 1], ALU.subtract, ALU.mult)
                ins.then_inc(norm2_ready, 1)

            def turn1_lo(c):
                for k in range(KD):
                    dve.wait_ge(t1_hi, c * KD + k + 1)
                    lo(xn1_lo[:, k, :], turn[k][:], xn1_hi[:, k, :]).then_inc(t1_lo, 1)

            def turn2_lo(f):
                for k in range(KD):
                    dve.wait_ge(t2_hi, f * KD + k + 1)
                    lo(xn2_lo[:, k, :], turn[k][:], xn2_hi[:, k, :]).then_inc(t2_lo, 1)

            def tap(a, j, t):
                if t == 1:
                    dve.wait_ge(tap_first, a * JD + j + 1)
                else:
                    dve.wait_ge(tap_added, a * JD * HALO + j // 2 * 2 * HALO + (t - 2) * 2 + j % 2 + 1)
                cols = conv[:, j, HALO - t:HALO - t + CH]
                nc.vector.scalar_tensor_tensor(cols, blk[j][:], tap_w[:, j, t:t + 1], cols, ALU.mult,
                                               ALU.add).then_inc(tap_added, 1)

            def taps(a, pair):
                for t in range(1, TAPS):
                    tap(a, 2 * pair, t)
                    tap(a, 2 * pair + 1, t)

            def hidden_lo(f):
                for j in range(JF):
                    dve.wait_ge(g_hi, f * JF + j + 1)
                    lo(hid_lo[:, j, :], hid[:, j, :], hid_hi[:, j, :]).then_inc(g_lo, 1)

            def edge(c, opens):
                if opens:
                    src = tap_b[:].rearrange("p (j o) -> p j o", o=1).broadcast_to([P, JD, HALO])
                else:
                    src = conv[:, :, CH:CH + HALO]
                if not (isinstance(c, int) and c == 0):
                    dve.wait_ge(xc_lo_set, c * JD)
                nc.vector.tensor_copy(conv[:, :, 0:HALO], src).then_inc(edge_set, 1)

            def scan(a, qa):
                dve.wait_ge(u_ready, a + 1)
                start = 0.0 if qa == 0 else state[:, 0, CH - 1:CH]
                nc.vector.tensor_tensor_scan(state[:, qa, :], decay[:], tok[1][:], start, ALU.mult,
                                             ALU.add).then_inc(scanned, 1)

            def state_lo(a, qa):
                dve.wait_ge(h_hi, a + 1)
                lo(state_mix[P // 2:P, :], state[P // 2:P, qa, :], state_mix[P // 2:P, :]).then_inc(h_lo, 1)

            def ys(a, js=range(JD)):
                for j in js:
                    dve.wait_ge(c_ready, a * JD + j + 1)
                    nc.vector.tensor_tensor(gate[:, j, :], blk[j][:], gate[:, j, :], ALU.mult).then_inc(y_set, 1)

            def finish(f, q, h):
                dve.wait_ge(down_ready, f * 2 + h + 1)
                dve.wait_ge(b2_added, f + 1)
                rows = x_mid[:, q, 2 * h:2 * h + 2, :].rearrange("p n d -> p (n d)")
                nc.vector.scalar_tensor_tensor(rows, tok[h][:], 1.0 / TOP_K, rows, ALU.mult, ALU.add).then_inc(done, 1)

            def route(seq):
                dve.wait_ge(late_loaded, 48)
                dve.wait_ge(scored, seq + 1)
                nc.vector.tensor_tensor(scores[:], tok[0][0:1, 0:E], b_router[:], ALU.add).then_inc(route_step, 1)
                dve.wait_ge(route_step, seq * 3 + 1)
                dve.sem_inc(passed, 1)
                nc.vector.max(best[:], scores[:]).then_inc(route_step, 1)
                dve.wait_ge(route_step, seq * 3 + 2)
                dve.sem_inc(passed, 1)
                nc.vector.max_index(expert[:], best[:], scores[:]).then_inc(route_step, 1)

            def read_choice(seq, t):
                if t == 0:
                    dve.wait_ge(e_loaded, 48)
                    dve.wait_ge(route_step, seq * 3 + 3)
                    dve.sem_inc(passed, 1)
                return nc.vector.value_load(expert[0:1, t:t + 1], min_val=0, max_val=E - 1)

            def choose_w1(seq, e, t):
                dve.wait_ge(w1_hi_set, seq * TOP_K + t + 1)
                lo(w1_lo[:, t, :], w1_all[:, bass.ds(e, 1), :].rearrange("p o c -> p (o c)"),
                   w1_hi[:, t, :]).then_inc(w1_lo_set, 1)

            def choose_b1(seq, chosen):
                for t, e in enumerate(chosen):
                    ins = nc.vector.tensor_copy(b1_sel[:, t, :], b1_all[:, bass.ds(e, 1), :].rearrange("p o k -> p (o k)"))
                ins.then_inc(b1_set, 1)

            def prologue():
                stats1(0)
                dve.wait_ge(w_hi_set, 1)
                lo(w_in_lo[:, :, 0:DI], raw_in[:, :, 0:DI], w_in_hi[:, :, 0:DI]).then_inc(w_lo_set, 1)
                turn1_lo(0)
                dve.wait_ge(taps_loaded, 32)
                edge(0, True)
                stats1(1)
                dve.wait_ge(w_hi_set, 4 + REP)
                for r in range(REP):
                    lo(b_mix[:, :, (2 * r + 1) * NST:(2 * r + 2) * NST], wb_raw[:],
                       b_mix[:, :, 2 * r * NST:(2 * r + 1) * NST]).then_inc(w_lo_set, 1)
                taps(0, 0)
                taps(0, 1)
                for r in (P // 4, 3 * P // 4):
                    rows = slice(r, r + P // 4)
                    lo(c_mix[rows, :], state[rows, 0, :], c_mix[rows, :]).then_inc(w_lo_set, 1)
                edge(1, False)
                dve.wait_ge(consts_set, 4)
                scan(0, 0)
                state_lo(0, 0)
                ys(0, (0,))
                turn1_lo(1)
                ys(0, range(1, JD))

            def step(f, q, seq, more):
                a, qa = f + 1, 1 - q
                taps(a, 0)
                tap(a, 2, 1)
                tap(a, 3, 1)
                residual(f, q, seq, 0)
                tap(a, 2, 2)
                if q == 0:
                    stats2(f, q, 0, (lambda: tap(a, 3, 2), None))
                    tap(a, 2, 3)
                    norm2(f, q, 0)
                    tap(a, 3, 3)
                else:
                    stats2(f, q, 0, (lambda: tap(a, 3, 2), lambda: tap(a, 2, 3)))
                    tap(a, 3, 3)
                    norm2(f, q, 0)
                residual(f, q, seq, 1)
                stats2(f, q, 1)
                if q == 0:
                    route(seq)
                norm2(f, q, 1)
                if q == 0:
                    first = read_choice(seq, 0)
                    choose_w1(seq, first, 0)
                turn2_lo(f)
                scan(a, qa)
                if q == 0:
                    second = read_choice(seq, 1)
                    choose_w1(seq, second, 1)
                    choose_b1(seq, (first, second))
                state_lo(a, qa)
                if more:
                    edge(a + 1, qa == 1)
                    stats1(a + 1)
                hidden_lo(f)
                ys(a)
                if more:
                    turn1_lo(a + 1)
                finish(f, q, 0)
                if not more:
                    for j in range(JD):
                        dve.wait_ge(y_hi_set, a * JD + j + 1)
                        lo(y_lo[:, j, :], gate[:, j, :], y_hi[:, j, :]).then_inc(y_lo_set, 1)
                finish(f, q, 1)

            def epilogue():
                f = NC - 1

                def turn2_half_lo(h):
                    dve.wait_ge(half_t2_hi, h + 1)
                    lo(xn2_lo[:, :, half_cols(h)], half_turn(h), xn2_hi[:, :, half_cols(h)]).then_inc(half_t2_lo, 1)

                def hidden_half_lo(h, js):
                    for j in js:
                        dve.wait_ge(half_g_hi, h * JF + j + 1)
                        lo(hid_lo[:, j, half_cols(h)], hid[:, j, half_cols(h)],
                           hid_hi[:, j, half_cols(h)]).then_inc(half_g_lo, 1)

                residual(f, 1, NC // 2 - 1, 0)
                stats2(f, 1, 0)
                norm2(f, 1, 0)
                residual(f, 1, NC // 2 - 1, 1)
                stats2(f, 1, 1)
                turn2_half_lo(0)
                norm2(f, 1, 1)
                hidden_half_lo(0, (0, 1))
                turn2_half_lo(1)
                hidden_half_lo(0, (2, 3))
                hidden_half_lo(1, range(JF))
                finish(f, 1, 0)
                finish(f, 1, 1)

            steps(dve, prologue, step, epilogue)

        @block.tensor
        def _(pe):
            mm = nc.tensor.matmul

            def turns(tiles, sem_out):
                for k in range(KD):
                    for t in tiles:
                        ins = nc.tensor.transpose(turn[k][:, t * P:(t + 1) * P], normed[:, t, k * P:(k + 1) * P],
                                                  ident[:])
                    if sem_out is not None:
                        ins.then_inc(sem_out, 1)
                return ins

            def turns1(c):
                pe.wait_ge(norm1_ready, c + 1)
                turns(range(TT), turned1)

            def project(j, whi, wlo, his, los, ready, c, sem_out):
                dst = blk[j][:]
                for k in range(KD):
                    if ready is not None:
                        pe.wait_ge(ready[0], c * KD + k + 1)
                    mm(dst, whi(k), his(k), start=(k == 0), stop=False)
                    mm(dst, wlo(k), his(k), start=False, stop=False)
                for k in range(KD):
                    if ready is not None:
                        pe.wait_ge(ready[1], c * KD + k + 1)
                    ins = mm(dst, whi(k), los(k), start=False, stop=(k == KD - 1))
                ins.then_inc(sem_out, 1)

            def in_proj(a, j, part, sem_out):
                cols = slice(part * DI + j * P, part * DI + (j + 1) * P)
                project(j, lambda k: w_in_hi[:, k, cols], lambda k: w_in_lo[:, k, cols],
                        lambda k: xn1_hi[:, k, :], lambda k: xn1_lo[:, k, :],
                        (t1_hi, t1_lo) if part == 0 and j == 0 else None, a, sem_out)

            def xp(a):
                for j in range(JD):
                    if not (isinstance(a, int) and a == 0):
                        pe.wait_ge(y_set, a * JD - JD + j + 1)
                    in_proj(a, j, 0, xp_ready)

            def z(a, j):
                pe.wait_ge(tap_added, a * JD * HALO + (j // 2) * 2 * HALO + 2 * (HALO - 1) + j % 2 + 1)
                in_proj(a, j, 1, z_ready)

            def up(f, q, seq):
                for j in range(JF):
                    if q == 0 and j % KD == 0:
                        pe.wait_ge(w1_lo_set, seq * TOP_K + j // KD + 1)
                    pe.wait_ge(gate_set, f * JD + JD + j + 1)
                    t, m = j // KD, j % KD
                    project(j, lambda k: w1_hi[:, t, k * D + m * P:k * D + (m + 1) * P],
                            lambda k: w1_lo[:, t, k * D + m * P:k * D + (m + 1) * P],
                            lambda k: xn2_hi[:, k, :], lambda k: xn2_lo[:, k, :],
                            (t2_hi, t2_lo) if j == 0 else None, f, up_ready)

            def tokens(h, j, last, his, los, whi, wlo):
                for n in range(2):
                    rows = slice((2 * h + n) * P, (2 * h + n + 1) * P)
                    dst = tok[h][:, n * D:(n + 1) * D]
                    mm(dst, his[:, j, rows], whi, start=(j == 0 and n == 0), stop=False, skip_group_check=True)
                    mm(dst, his[:, j, rows], wlo, start=False, stop=False, skip_group_check=True)
                    ins = mm(dst, los[:, j, rows], whi, start=False, stop=(last and n == 1), skip_group_check=True)
                return ins

            def down(f, h, js=range(JF)):
                for j in js:
                    if h == 0:
                        pe.wait_ge(g_lo, f * JF + j + 1)
                    t, cols = j // KD, slice(j % KD * D, (j % KD + 1) * D)
                    ins = tokens(h, j, j == JF - 1, hid_hi, hid_lo, w2_hi[:, t, cols], w2_lo[:, t, cols])
                if js[-1] == JF - 1:
                    ins.then_inc(down_ready, 1)

            def out_proj(f, h):
                pe.wait_ge(done, f * 2 + h + 1)
                for j in range(JD):
                    if h == 0:
                        pe.wait_ge(y_lo_set, f * JD + j + 1)
                    ins = tokens(h, j, j == JD - 1, y_hi, y_lo, w_out_hi[:, j, :], w_out_lo[:, j, :])
                ins.then_inc(mixed, 1)

            def state_in_hi(a):
                for j in range(JD):
                    pe.wait_ge(xc_hi_set, a * JD + j + 1)
                    mm(tok[1][:], b_mix[:, j, :], xc_hi[:, j, :], start=(j == 0), stop=False)

            def state_in_lo(a):
                for j in range(JD):
                    pe.wait_ge(xc_lo_set, a * JD + j + 1)
                    ins = mm(tok[1][:], b_mix[:, j, :], xc_lo[:, j, :], start=False, stop=(j == JD - 1))
                ins.then_inc(u_ready, 1)

            def state_out(a, js):
                pe.wait_ge(h_lo, a + 1)
                for j in js:
                    if not (isinstance(a, int) and a == 0):
                        pe.wait_ge(gelu_set, (a - 1) * JF + j + 1)
                    mm(blk[j][:], c_mix[:, j * P:(j + 1) * P], state_mix[:], start=True,
                       stop=True).then_inc(c_ready, 1)

            def prologue():
                pe.wait_ge(consts_set, 4)
                turns1(0)
                pe.wait_ge(w_lo_set, 1)
                xp(0)
                pe.wait_ge(z_out_lo_set, 1)
                for j in range(JD):
                    z(0, j)
                    if j == 1:
                        turns1(1)
                pe.wait_ge(w_lo_set, 3 + REP)
                state_in_hi(0)
                state_in_lo(0)
                pe.wait_ge(gate_set, JD)
                state_out(0, range(JD))
                pe.wait_ge(z_out_lo_set, 2)
                pe.wait_ge(late_loaded, 48)

            def step(f, q, seq, more):
                a = f + 1
                xp(a)
                out_proj(f, 0)
                out_proj(f, 1)
                z(a, 0)
                z(a, 1)
                if q == 1:
                    z(a, 2)
                pe.wait_ge(norm2_ready, f * 2 + 1)
                ins = turns(range(2), None)
                if q == 0:
                    ins.then_inc(turned_first, 1)
                    z(a, 2)
                    pe.wait_ge(first_set, seq * KD + KD)
                    for k in range(KD):
                        ins = mm(tok[0][0:1, 0:E], first_tok[:, k:k + 1], w_router[:, k, :], start=(k == 0),
                                 stop=(k == KD - 1))
                    ins.then_inc(scored, 1)
                z(a, 3)
                pe.wait_ge(mid_set, f * 2 + 2)
                state_in_hi(a)
                pe.wait_ge(norm2_ready, f * 2 + 2)
                turns(range(2, TT), turned2)
                state_in_lo(a)
                up(f, q, seq)
                state_out(a, range(JD - 1))
                if q == 0:
                    pe.wait_ge(w2_lo_set, seq * TOP_K + TOP_K)
                down(f, 0, (0,))
                state_out(a, (JD - 1,))
                down(f, 0, range(1, JF))
                if more:
                    turns1(a + 1)
                down(f, 1)

            def epilogue():
                f = NC - 1
                out_proj(f, 0)
                out_proj(f, 1)
                pe.wait_ge(y_set, NC * JD)

                def turn_half(h):
                    pe.wait_ge(norm2_ready, f * 2 + h + 1)
                    for k in range(KD):
                        for t in range(2):
                            ins = nc.tensor.transpose(half_turn(h)[:, k, t * P:(t + 1) * P],
                                                      normed[:, 2 * h + t, k * P:(k + 1) * P], ident[:])
                    ins.then_inc(half_turned, 1)

                def up_half(h, j):
                    t, dst, cols = j // KD, half_blk(h, j), half_cols(h)
                    his = [w1_hi[:, t, k * D + j % KD * P:k * D + (j % KD + 1) * P] for k in range(KD)]
                    los = [w1_lo[:, t, k * D + j % KD * P:k * D + (j % KD + 1) * P] for k in range(KD)]
                    pe.wait_ge(half_t2_hi, h + 1)
                    for k in range(KD):
                        mm(dst, his[k], xn2_hi[:, k, cols], start=(k == 0), stop=False)
                        mm(dst, los[k], xn2_hi[:, k, cols], start=False, stop=False)
                    pe.wait_ge(half_t2_lo, h + 1)
                    for k in range(KD):
                        ins = mm(dst, his[k], xn2_lo[:, k, cols], start=False, stop=(k == KD - 1))
                    ins.then_inc(half_up, 1)

                turn_half(0)
                up_half(0, 0)
                up_half(0, 1)
                turn_half(1)
                up_half(0, 2)
                up_half(0, 3)
                for j in range(JF):
                    up_half(1, j)
                for h in range(2):
                    for j in range(JF):
                        pe.wait_ge(half_g_lo, h * JF + j + 1)
                        t, cols = j // KD, slice(j % KD * D, (j % KD + 1) * D)
                        ins = tokens(h, j, j == JF - 1, hid_hi, hid_lo, w2_hi[:, t, cols], w2_lo[:, t, cols])
                    ins.then_inc(down_ready, 1)

            steps(pe, prologue, step, epilogue)


_INS = ["L0_attn_x", "L0_attn_w_in", "L0_attn_conv_w", "L0_attn_conv_b", "L0_attn_w_B", "L0_attn_w_C",
        "L0_attn_w_out", "L0_ffn_Wr", "L0_ffn_br", "L0_ffn_W1", "L0_ffn_b1", "L0_ffn_W2", "L0_ffn_b2"]


def kernel(**inputs):
    import numpy as _np
    import concourse.bacc as _bacc
    from concourse import mybir as _mybir
    from concourse.bass_utils import run_bass_kernel_spmd as _run

    nc = _bacc.Bacc("TRN2", target_bir_lowering=False, num_devices=1)
    arrays, args = {}, []
    for name in _INS:
        a = _np.ascontiguousarray(inputs[name])
        arrays[f"in_{name}"] = a
        args.append(nc.dram_tensor(f"in_{name}", a.shape, _mybir.dt.from_np(a.dtype), kind="ExternalInput").ap())
    shape = inputs["L0_attn_x"].shape
    args.append(nc.dram_tensor("out_0", shape, F32, kind="ExternalOutput").ap())
    build_block(nc, *args)
    r = _run(nc, [arrays], core_ids=[0])
    return r.results[0]["out_0"]
```
